# Optimizing a Trainium2 kernel written in Bass

```python
import numpy as np
import jax
import jax.numpy as jnp

def _softmax(x, axis=-1):
    return jax.nn.softmax(x, axis=axis)

def _gelu(x):
    return jax.nn.gelu(x, approximate=True)

def _silu(x):
    return jax.nn.silu(x)

def _sigmoid(x):
    return jax.nn.sigmoid(x)

def _layernorm(x, axis=-1, eps=1e-05):
    m = jnp.mean(x, axis=axis, keepdims=True)
    v = jnp.var(x, axis=axis, keepdims=True)
    return (x - m) / jnp.sqrt(v + eps)

def _scatter_add(tgt, idx, src, axis=0):
    return tgt.at[idx].add(src)

def _segment_sum(src, seg, n):
    return jax.ops.segment_sum(src, seg, n)
kernel_name = 'mk_perceiver_d1_seqx_r2_65d08a'

def setup_inputs(seed: int=0):
    np.random.seed(seed)
    _w = jnp.asarray

    def _rec_inputs():
        import jax
        import jax.numpy as jnp
        _rk = jax.random.key(seed)
        x = 7.22e-05 + 1 * jax.random.normal(jax.random.fold_in(_rk, 1), (16, 64, 512), jnp.float32)
        _lenS = 64 - jax.random.randint(jax.random.fold_in(_rk, 7), (16,), 0, max(1, 64 // 4) + 1, jnp.int32)
        _lenS2 = 1601 - jax.random.randint(jax.random.fold_in(_rk, 8), (16,), 0, max(1, 1601 // 4) + 1, jnp.int32)
        _ctx_1024P = jax.random.normal(jax.random.fold_in(_rk, 11), (16, 16, 512), jnp.float32)
        _ctx_1024c = jax.random.dirichlet(jax.random.fold_in(_rk, 511), 0.3 * jnp.ones((16,), jnp.float32), (16, 1601))
        _ctx_1024t = jnp.einsum('bsk,bkd->bsd', _ctx_1024c, _ctx_1024P)
        _ctx_1024t = _ctx_1024t * jax.lax.rsqrt(jnp.mean(jnp.square(_ctx_1024t)) + 1e-12) * 0.953939
        ctx_1024 = 4.13588e-05 + 0.999923 * (_ctx_1024t + 0.3 * jax.random.normal(jax.random.fold_in(_rk, 611), (16, 1601, 512), jnp.float32))
        return (x, ctx_1024)
    x, ctx_1024 = _rec_inputs()

    def _L0_xattn_setup():
        import jax, jax.numpy as jnp
        import numpy as np
        B, SQ, SK, D = (4, 1024, 1024, 512)
        key = jax.random.key(seed)
        ks = jax.random.split(key, 8)
        s = 1.0 / np.sqrt(D)
        return {'input_seq': jax.random.normal(ks[0], (B, SQ, D), jnp.float32), 'condition_seq': jax.random.normal(ks[1], (B, SK, D), jnp.float32), 'Wq': jax.random.normal(ks[2], (D, D), jnp.float32) * s, 'bq': jnp.zeros((D,), jnp.float32), 'Wk': jax.random.normal(ks[3], (D, D), jnp.float32) * s, 'bk': jnp.zeros((D,), jnp.float32), 'Wv': jax.random.normal(ks[4], (D, D), jnp.float32) * s, 'bv': jnp.zeros((D,), jnp.float32)}
    _L0_xattn_all = _L0_xattn_setup()
    _L0_xattn_in = {k: v for k, v in _L0_xattn_all.items() if k in ('Wq', 'bq', 'Wk', 'bk', 'Wv', 'bv')}
    del _L0_xattn_all

    def _L0_attn_setup():
        import jax, jax.numpy as jnp
        import numpy as np
        EPS_RHO = 1e-08
        EPS_DEN = 1e-09

        def _rho_signed_sqrt(x):
            return jnp.sqrt(jax.nn.relu(x) + EPS_RHO) - jnp.sqrt(jax.nn.relu(-x) + EPS_RHO)
        key = jax.random.key(seed)
        ks = jax.random.split(key, 8)
        B, N, C, A = (2, 256, 512, 64)
        s_c = 1.0 / np.sqrt(C)
        s_a = 1.0 / np.sqrt(A)
        return {'X': jax.random.normal(ks[0], (B, N, C), jnp.float32), 'Wq': jax.random.normal(ks[1], (A, C), jnp.float32) * s_c, 'Wk': jax.random.normal(ks[2], (A, C), jnp.float32) * s_c, 'Wphi': jax.random.normal(ks[3], (A,), jnp.float32) * s_a, 'Wy_w': jax.random.normal(ks[4], (C, C), jnp.float32) * s_c, 'Wy_b': jax.random.normal(ks[5], (C,), jnp.float32) * s_c, 'We_w': jax.random.normal(ks[6], (C, A), jnp.float32) * s_a, 'We_b': jax.random.normal(ks[7], (C,), jnp.float32) * s_a}
    _L0_attn_all = _L0_attn_setup()
    _L0_attn_in = {k: v for k, v in _L0_attn_all.items() if k in ('Wq', 'Wk', 'Wphi', 'Wy_w', 'Wy_b', 'We_w', 'We_b')}
    del _L0_attn_all

    def _L0_ffn_setup():
        import jax, jax.numpy as jnp
        import numpy as np
        H = 512
        I = 256
        E = 8
        TOPK = 2
        NGROUP = 4
        TOPKG = 2
        SCALE = 1.0
        B, S = (4, 512)

        def _gate(xf, gate_weight, bias):
            T = xf.shape[0]
            logits = xf @ gate_weight.T
            scores = jax.nn.sigmoid(logits)
            scores_for_choice = scores + bias[None, :]
            gsz = E // NGROUP
            grp = scores_for_choice.reshape(T, NGROUP, gsz)
            group_scores = jax.lax.top_k(grp, 2)[0].sum(-1)
            _, group_idx = jax.lax.top_k(group_scores, TOPKG)
            rows = jnp.arange(T)[:, None]
            group_mask = jnp.zeros((T, NGROUP), xf.dtype).at[rows, group_idx].set(1.0)
            score_mask = jnp.broadcast_to(group_mask[:, :, None], (T, NGROUP, gsz)).reshape(T, E)
            tmp_scores = jnp.where(score_mask > 0, scores_for_choice, 0.0)
            _, topk_idx = jax.lax.top_k(tmp_scores, TOPK)
            topk_weight = jnp.take_along_axis(scores, topk_idx, axis=1)
            if TOPK > 1:
                topk_weight = topk_weight / (topk_weight.sum(-1, keepdims=True) + 1e-20)
            topk_weight = topk_weight * SCALE
            return (topk_idx, topk_weight)
        key = jax.random.key(seed)
        k0, k1, k2, k3, k4 = jax.random.split(key, 5)
        return {'hidden_states': jax.random.normal(k0, (B, S, H), jnp.float32), 'gate_weight': jax.random.normal(k1, (E, H), jnp.float32) * (1.0 / np.sqrt(H)), 'e_score_correction_bias': jnp.zeros((E,), jnp.float32), 'gate_proj': jax.random.normal(k2, (E, I, H), jnp.float32) * 0.02, 'up_proj': jax.random.normal(k3, (E, I, H), jnp.float32) * 0.02, 'down_proj': jax.random.normal(k4, (E, H, I), jnp.float32) * 0.02}
    _L0_ffn_all = _L0_ffn_setup()
    _L0_ffn_in = {k: v for k, v in _L0_ffn_all.items() if k in ('gate_weight', 'e_score_correction_bias', 'gate_proj', 'up_proj', 'down_proj')}
    del _L0_ffn_all
    return {'x': x, 'ctx_1024': ctx_1024, 'L0_xattn_Wq': _L0_xattn_in['Wq'], 'L0_xattn_bq': _L0_xattn_in['bq'], 'L0_xattn_Wk': _L0_xattn_in['Wk'], 'L0_xattn_bk': _L0_xattn_in['bk'], 'L0_xattn_Wv': _L0_xattn_in['Wv'], 'L0_xattn_bv': _L0_xattn_in['bv'], 'L0_attn_Wq': _L0_attn_in['Wq'], 'L0_attn_Wk': _L0_attn_in['Wk'], 'L0_attn_Wphi': _L0_attn_in['Wphi'], 'L0_attn_Wy_w': _L0_attn_in['Wy_w'], 'L0_attn_Wy_b': _L0_attn_in['Wy_b'], 'L0_attn_We_w': _L0_attn_in['We_w'], 'L0_attn_We_b': _L0_attn_in['We_b'], 'L0_ffn_gate_weight': _L0_ffn_in['gate_weight'], 'L0_ffn_e_score_correction_bias': _L0_ffn_in['e_score_correction_bias'], 'L0_ffn_gate_proj': _L0_ffn_in['gate_proj'], 'L0_ffn_up_proj': _L0_ffn_in['up_proj'], 'L0_ffn_down_proj': _L0_ffn_in['down_proj']}

def reference(x, ctx_1024, L0_xattn_Wq, L0_xattn_bq, L0_xattn_Wk, L0_xattn_bk, L0_xattn_Wv, L0_xattn_bv, L0_attn_Wq, L0_attn_Wk, L0_attn_Wphi, L0_attn_Wy_w, L0_attn_Wy_b, L0_attn_We_w, L0_attn_We_b, L0_ffn_gate_weight, L0_ffn_e_score_correction_bias, L0_ffn_gate_proj, L0_ffn_up_proj, L0_ffn_down_proj):
    import jax
    import jax.numpy as jnp

    def _L0_xattn_ref(input_seq, condition_seq, Wq, bq, Wk, bk, Wv, bv):
        import jax, jax.numpy as jnp
        import numpy as np
        B, SQ, SK, D = (4, 1024, 1024, 512)
        q = jnp.einsum('bsd,ed->bse', input_seq, Wq) + bq
        k = jnp.einsum('btd,ed->bte', condition_seq, Wk) + bk
        v = jnp.einsum('btd,ed->bte', condition_seq, Wv) + bv
        scores = jnp.einsum('bse,bte->bst', q, k)
        attn = jax.nn.softmax(scores, axis=-1)
        attended = jnp.einsum('bst,bte->bse', attn, v)
        return attended

    def _L0_attn_ref(X, Wq, Wk, Wphi, Wy_w, Wy_b, We_w, We_b):
        import jax, jax.numpy as jnp
        import numpy as np
        EPS_RHO = 1e-08
        EPS_DEN = 1e-09

        def _rho_signed_sqrt(x):
            return jnp.sqrt(jax.nn.relu(x) + EPS_RHO) - jnp.sqrt(jax.nn.relu(-x) + EPS_RHO)
        q = jnp.einsum('bnc,ac->bna', X, Wq)
        k = jnp.einsum('bnc,ac->bna', X, Wk)
        Vy = jnp.einsum('bnc,dc->bnd', X, Wy_w) + Wy_b
        e = jax.nn.relu(_rho_signed_sqrt(q[:, :, None, :] + k[:, None, :, :]))
        scores = jnp.einsum('bija,a->bij', e, Wphi)
        m = jnp.max(scores, axis=-1, keepdims=True)
        ex = jnp.exp(scores - m)
        denom = jnp.sum(ex, axis=-1)
        part1 = jnp.einsum('bij,bjc->bic', ex, Vy)
        Ew = jnp.einsum('bij,bija->bia', ex, e)
        part2 = jnp.einsum('bia,ca->bic', Ew, We_w) + We_b * denom[..., None]
        return (part1 + part2) / (denom[..., None] + EPS_DEN)

    def _L0_ffn_ref(hidden_states, gate_weight, e_score_correction_bias, gate_proj, up_proj, down_proj):
        import jax, jax.numpy as jnp
        import numpy as np
        H = 512
        I = 256
        E = 8
        TOPK = 2
        NGROUP = 4
        TOPKG = 2
        SCALE = 1.0
        B, S = (4, 512)

        def _gate(xf, gate_weight, bias):
            T = xf.shape[0]
            logits = xf @ gate_weight.T
            scores = jax.nn.sigmoid(logits)
            scores_for_choice = scores + bias[None, :]
            gsz = E // NGROUP
            grp = scores_for_choice.reshape(T, NGROUP, gsz)
            group_scores = jax.lax.top_k(grp, 2)[0].sum(-1)
            _, group_idx = jax.lax.top_k(group_scores, TOPKG)
            rows = jnp.arange(T)[:, None]
            group_mask = jnp.zeros((T, NGROUP), xf.dtype).at[rows, group_idx].set(1.0)
            score_mask = jnp.broadcast_to(group_mask[:, :, None], (T, NGROUP, gsz)).reshape(T, E)
            tmp_scores = jnp.where(score_mask > 0, scores_for_choice, 0.0)
            _, topk_idx = jax.lax.top_k(tmp_scores, TOPK)
            topk_weight = jnp.take_along_axis(scores, topk_idx, axis=1)
            if TOPK > 1:
                topk_weight = topk_weight / (topk_weight.sum(-1, keepdims=True) + 1e-20)
            topk_weight = topk_weight * SCALE
            return (topk_idx, topk_weight)
        Bv, Sv, Hv = hidden_states.shape
        xf = hidden_states.reshape(-1, Hv).astype(jnp.float32)
        topk_idx, topk_weight = _gate(xf, gate_weight.astype(jnp.float32), e_score_correction_bias.astype(jnp.float32))
        y = jnp.zeros_like(xf)
        for e in range(E):
            combine_w = jnp.where(topk_idx == e, topk_weight, 0.0).sum(-1)
            g = xf @ gate_proj[e].T
            u = xf @ up_proj[e].T
            o = jax.nn.silu(g) * u @ down_proj[e].T
            y = y + combine_w[:, None] * o
        return y.reshape(Bv, Sv, Hv)
    x = x + _L0_xattn_ref(_layernorm(x, axis=-1), ctx_1024, L0_xattn_Wq, L0_xattn_bq, L0_xattn_Wk, L0_xattn_bk, L0_xattn_Wv, L0_xattn_bv)
    x = x + _L0_attn_ref(_layernorm(x, axis=-1), L0_attn_Wq, L0_attn_Wk, L0_attn_Wphi, L0_attn_Wy_w, L0_attn_Wy_b, L0_attn_We_w, L0_attn_We_b)
    x = x + _L0_ffn_ref(_layernorm(x, axis=-1), L0_ffn_gate_weight, L0_ffn_e_score_correction_bias, L0_ffn_gate_proj, L0_ffn_up_proj, L0_ffn_down_proj)
    return x

_drawn_inputs = setup_inputs


def setup_inputs(seed=0):
    import zlib

    import numpy as np

    out = dict(_drawn_inputs(seed))
    spreads = {'L0_xattn_bq': (0.0, 0.1),
     'L0_xattn_bk': (0.0, 0.8),
     'L0_xattn_bv': (0.0, 0.1),
     'L0_ffn_e_score_correction_bias': (0.0, 0.8)}
    factors = {'L0_ffn_gate_weight': 4.844,
     'L0_ffn_gate_proj': 4.218,
     'L0_ffn_up_proj': 4.13,
     'L0_ffn_down_proj': 4.115}
    for name, (base, spread) in spreads.items():
        noise = np.random.default_rng([zlib.crc32(name.encode()), seed]).standard_normal(out[name].shape)
        drawn = base * np.exp(spread * noise) if base else spread * noise
        out[name] = jnp.asarray(drawn.astype(out[name].dtype))
    for name, factor in factors.items():
        out[name] = (out[name] * factor).astype(out[name].dtype)
    return out
```

```python
from contextlib import ExitStack

import concourse.bass as bass
from concourse import mybir

F32 = mybir.dt.float32
F32R = mybir.dt.float32r
ALU = mybir.AluOpType
ACT = mybir.ActivationFunctionType
AX = mybir.AxisListType
ds = bass.ds

LN_EPS = 1e-5
EPS_RHO = 1e-8
ROOT_EPS_RHO = 1e-4
EPS_DEN = 1e-9
EPS_TOPK = 1e-20

P = 128


def perceiver_kernel(nc, x, ctx, ctx_t, wq, bq, wk, bk, wv_t, bv, wqk_t, wphi, wy_t, wy_b, we_t, we_b,
                     gate_t, gate_bias, gu_t, down_t, out):
    B, SQ, D = x.shape
    SK = ctx.shape[1]
    A = wphi.shape[0]
    E, _, I2 = gu_t.shape
    I = I2 // 2
    KD = D // P
    NP = B * SQ // P
    BP = P // SQ
    NCH = 4
    CW = -(-SK // NCH)
    NT = -(-SK // P)
    TAIL = SK - (NT - 1) * P
    GROUPS = [(0, 4), (4, 7), (7, 10), (10, 13)]
    RING = 10
    NC8 = SQ * SQ // 512
    LOW = 8
    POOL_CONSTS = 14
    assert (B, SQ, D, A, NT, I) == (16, 64, 512, 64, 13, 256) and BP == 2

    def width(c):
        return min(CW, SK - c * CW)

    x_pairs = x.rearrange("(p b) s d -> p (b s) d", b=BP)
    out_rows = out.rearrange("b s d -> (b s) d").rearrange("(t p) d -> t p d", p=P)
    ctx_flat = ctx.rearrange("b t d -> (b t) d")
    ctx_t_rows = ctx_t.rearrange("b (k p) t -> p (b k) t", p=P)

    with ExitStack() as stack:
        base = (nc.sbuf_base + 63) // 64 * 64
        cursor = [base]

        def place(name, shape, dt=F32, at=None):
            n = 4
            for s in shape[1:]:
                n *= s
            where = cursor[0] if at is None else at
            if at is None:
                cursor[0] += (n + 31) // 32 * 32
            return nc.alloc_sbuf_tensor_at(name, shape, dt, offset=where)

        def region(nbytes):
            where = cursor[0]
            cursor[0] += nbytes
            return where

        at_keys = region(NCH * BP * KD * CW * 4)
        keys = place("keys", [P, NCH, BP * KD, CW], at=at_keys)
        WSZ = KD * I2 + (I // P) * D
        w_hi = [place(f"w_hi{s}", [P, WSZ], F32R, at=at_keys + s * 2 * WSZ * 4) for s in range(2)]
        w_lo = [place(f"w_lo{s}", [P, WSZ], F32R, at=at_keys + (s * 2 + 1) * WSZ * 4) for s in range(2)]
        x1t_lo2 = place("x1t_lo2", [P, KD, 512], F32R, at=at_keys + (NCH - 1) * BP * KD * CW * 4)
        at_vals = region(BP * RING * D * 4)
        vals = place("vals", [P, RING, BP, D], at=at_vals)
        wq_sb = place("wq_sb", [P, KD, D], at=at_vals)
        wk_sb = place("wk_sb", [P, KD, D], at=at_vals + 8192)
        dn_raw = [place(f"dn_raw{s}", [P, I // P, D], at=at_vals + 32768 + 4096 * s) for s in range(2)]
        bq_rep = place("bq_rep", [P, KD, P], at=at_vals + 36864)
        bk_rep = place("bk_rep", [P, KD, P], at=at_vals + 32768)
        v_rep = place("v_rep", [P, D], at=at_vals + 34816)
        x3_hi = place("x3_hi", [P, KD, NP * P], F32R, at=at_vals)
        x3_lo = place("x3_lo", [P, KD, NP * P], F32R, at=at_vals + 16384)
        at_proj = region(4 * KD * D * 4)
        wv_hi = place("wv_hi", [P, KD, D], F32R, at=at_proj)
        wv_lo = place("wv_lo", [P, KD, D], F32R, at=at_proj + 8192)
        wv_raw = place("wv_raw", [P, KD, D], F32, at=at_proj + 8192)
        wy_hi = place("wy_hi", [P, KD, D], F32R, at=at_proj + 16384)
        wy_lo = place("wy_lo", [P, KD, D], F32R, at=at_proj + 24576)
        wy_raw = place("wy_raw", [P, KD, D], F32, at=at_proj + 24576)
        silu_sb = place("silu_sb", [P, 2, 512], at=at_proj)
        h_sb = place("h_sb", [P, 2, 512], at=at_proj + 4096)
        h_hi = [place(f"h_hi{s}", [P, 2, 512], F32R, at=at_proj + 8192 + s * 8192) for s in range(2)]
        gu_raw = [place("gu_raw0", [P, KD, I2], at=at_proj + 24576)]
        h_lo = [place(f"h_lo{s}", [P, 2, 512], F32R, at=at_proj + 12288 + s * 8192) for s in range(2)]
        at_plane = region(SQ * SQ * 4)
        plane = place("plane", [P, SQ * SQ], at=at_plane)
        x1t_hi = place("x1t_hi", [P, KD, 512], F32R, at=at_plane)
        x1t_lo = place("x1t_lo", [P, KD, 512], F32R, at=at_plane + 8192)
        n3 = [place(f"n3_{s}", [P, D], at=at_plane + 2048 * s) for s in range(2)]
        gate_hi = place("gate_hi", [P, KD, P], F32R, at=at_plane + 4096)
        gate_lo = place("gate_lo", [P, KD, P], F32R, at=at_plane + 6144)
        logit_t = place("logit_t", [E, NP * P], at=at_plane + 8192)
        beat = place("beat", [P, NP, E, E], at=at_plane + 12288)
        tie = place("tie", [P, NP, E, E], at=at_plane + 14336)
        rows = place("rows", [P, NP * D])
        rows3 = rows[:, :].rearrange("p (n d) -> p n d", d=D)
        at_probs = cursor[0]
        m_hi = place("m_hi", [P, KD, D], F32R, at=at_probs)
        m_lo = place("m_lo", [P, KD, D], F32R, at=at_probs + 8192)
        x1t_hi2 = place("x1t_hi2", [P, KD, 512], F32R, at=at_probs + 16384)
        probs = place("probs", [P, SK])
        gate_sb = place("gate_sb", [P, KD, P], at=cursor[0] - (SK * 4 + 31) // 32 * 32)
        probs_t = place("probs_t", [P, NT, P])
        at_late = [cursor[0] - NT * P * 4]
        x_in = place("x_in", [P, D])
        gu_raw.append(place("gu_raw1", [P, KD, I2], at=cursor[0] - 2048))
        norm = place("norm", [P, D])
        nt_hi = place("nt_hi", [P, KD, P], F32R)
        nt_lo = place("nt_lo", [P, KD, P], F32R)
        nt_f = place("nt_f", [P, KD, P])
        vy = place("vy", [P, D])
        assert cursor[0] >= at_probs + 24576
        q_cur = place("q_cur", [P, KD, P])
        bv_b = place("bv_b", [P, D])
        bwe_b = place("bwe_b", [P, D])
        we2 = place("we2", [P, D])
        wqk_sb = place("wqk_sb", [P, KD, P])
        sel = place("sel", [P, NC8, P], F32R)
        ex = place("ex", [P, 512])
        at_exs = region(4096)
        ex_hi = place("ex_hi", [P, 512], F32R, at=at_exs)
        ex_parts = place("ex_parts", [P, 512], F32R, at=at_exs + 2048)
        sel_f = place("sel_f", [P, NC8, P], at=at_exs)
        ex_t = place("ex_t", [P, P])
        ew_t = place("ew_t", [P, P])
        ew = place("ew", [P, SQ])
        ident = place("ident", [P, P])
        phi_sel = place("phi_sel", [P, 2, 32])
        tmp = place("tmp", [P, D])
        q2 = place("q2", [P, SQ])
        k2 = place("k2", [P, SQ])
        small = {}
        for name, n in (("ones", 2), ("bq_c", KD), ("bk_c", KD), ("kbias", KD), ("cq", NP), ("c0", 1), ("phi_c", 1),
                        ("low_rows", 16), ("minus_low", 1), ("eps_ln", 1), ("eps_rho", 1), ("mx", NCH), ("mx1", 1), ("smax", 1), ("ebias", 1),
                        ("sums", NCH), ("ssum", 1), ("rinv", 1), ("st3", 6 * NP), ("mv3", 2 * NP), ("sd3", NP), ("rs3", NP), ("st1", 6 * NP), ("mv1", 2 * NP), ("sd1", NP),
                        ("rs1", NP), ("st2", 6), ("mv2", 2), ("sd2", 1), ("rs2", 1), ("mx16", 8), ("den", 1),
                        ("den1", 1), ("rden", 1)):
            small[name] = place(name, [P, n])
        small["gbias"] = place("gbias", [P, E])
        small["before"] = place("before", [P, E * E])
        for name, n in (("logits", NP * E), ("score", NP * E), ("choice", NP * E),
                        ("grp", NP * E // 2), ("grank", NP * E // 2), ("gmask", NP * E // 2), ("kept", NP * E),
                        ("rank", NP * E), ("wsel", NP * E), ("wsum", NP), ("winv", NP), ("comb", E * NP),
                        ("comb_e0", NP), ("comb_e1", NP)):
            small[name] = place(name, [P, n], at=at_late[0])
            at_late[0] += (n * 4 + 31) // 32 * 32
        assert cursor[0] <= nc.sbuf_usable_end, cursor[0]

        ps = stack.enter_context(nc.psum_tensor("ps", [P, 8, 512], F32))
        TRA, TRB, OUT, ACC = 4, 5, 6, 7

        def sem(name):
            return stack.enter_context(nc.semaphore(name))

        x_all_in, bias_in = sem("x_all_in"), sem("bias_in")
        wqk_in = [sem(f"wqk_in{k}") for k in range(KD)]
        x_all_in2 = sem("x_all_in2")
        wv_in, wy_in, small_in = sem("wv_in"), sem("wy_in"), sem("small_in")
        keys_in = [sem(f"keys_in{c}") for c in range(NCH)]
        vals_in = [sem(f"vals_in{g}") for g in range(len(GROUPS))]
        x_in_sem = sem("x_in_sem")
        gu_in = [sem(f"gu_in{s}") for s in range(2)]
        dn_in = [sem(f"dn_in{s}") for s in range(2)]
        gate_in, gate_zero = sem("gate_in"), sem("gate_zero")
        out_done = sem("out_done")
        pool_const, bk_rep_ok, phi_ok, bwe_ok, vec_const = (sem("pool_const"), sem("bk_rep_ok"), sem("phi_ok"),
                                                            sem("bwe_ok"), sem("vec_const"))
        sel_ok, low_rows_ok = sem("sel_ok"), sem("low_rows_ok")
        m_mm, m_hi_ok, m_lo_ok, vrep_mm, bias_mm, bias_ok = (sem("m_mm"), sem("m_hi_ok"), sem("m_lo_ok"),
                                                             sem("vrep_mm"), sem("bias_mm"), sem("bias_ok"))
        ln1_stat, ln1_sd, ln1_rs, ln1_ok, ln1_tr, ln1_hi, ln1_lo, cq_ok = (
            sem("ln1_stat"), sem("ln1_sd"), sem("ln1_rs"), sem("ln1_ok"), sem("ln1_tr"), sem("ln1_hi"),
            sem("ln1_lo"), sem("cq_ok"))
        q_mm, q_ok = sem("q_mm"), sem("q_ok")
        wsplit_hi, wsplit_lo = sem("wsplit_hi"), sem("wsplit_lo")
        q_ready, xb_ready, scored, max_step, ebias_ok, exp_done = (sem("q_ready"), sem("xb_ready"), sem("scored"),
                                                                   sem("max_step"), sem("ebias_ok"), sem("exp_done"))
        probs_tr, pt_act, pt_dve, pv_done, rinv_step, attended_ok = (sem("probs_tr"), sem("pt_act"), sem("pt_dve"),
                                                                     sem("pv_done"), sem("rinv_step"),
                                                                     sem("attended_ok"))
        o_tr, o_hi, o_lo, vproj, x1_ok, ln2_stat, ln2_sd, ln2_rs, ln2_ok = (
            sem("o_tr"), sem("o_hi"), sem("o_lo"), sem("vproj"), sem("x1_ok"), sem("ln2_stat"), sem("ln2_sd"),
            sem("ln2_rs"), sem("ln2_ok"))
        n_tr, n_f, n_hi, n_lo, qk_mm, qk_ok, vy_mm, vy_ok = (sem("n_tr"), sem("n_f"), sem("n_hi"), sem("n_lo"),
                                                             sem("qk_mm"), sem("qk_ok"), sem("vy_mm"), sem("vy_ok"))
        z_dve, z_pool, relu_ok, root_ok, s16_mm, s16_max, s16_sub, s16_exp, ex_hi_ok, ex_parts_ok = (
            sem("z_dve"), sem("z_pool"), sem("relu_ok"), sem("root_ok"), sem("s16_mm"), sem("s16_max"),
            sem("s16_sub"), sem("s16_exp"), sem("ex_hi_ok"), sem("ex_parts_ok"))
        ex_tr, ex_t_ok, spread, prod, ew_red, ew_ok, den_mm, den_ok, rden_ok, part_mm, tmp_ok, x2_ok = (
            sem("ex_tr"), sem("ex_t_ok"), sem("spread"), sem("prod"), sem("ew_red"), sem("ew_ok"), sem("den_mm"),
            sem("den_ok"), sem("rden_ok"), sem("part_mm"), sem("tmp_ok"), sem("x2_ok"))
        st3_ok = sem("st3_ok")
        ln3_stat, ln3_sd, ln3_rs, ln3_ok, x3_tr, x3_hi_ok, x3_lo_ok = (
            sem("ln3_stat"), sem("ln3_sd"), sem("ln3_rs"), sem("ln3_ok"), sem("x3_tr"), sem("x3_hi_ok"),
            sem("x3_lo_ok"))
        gate_split_hi, gate_split_lo, logit_mm, logit_ok, logit_tr, logits_ok, score_ok, gate_step = (
            sem("gate_split_hi"), sem("gate_split_lo"), sem("logit_mm"), sem("logit_ok"), sem("logit_tr"),
            sem("logits_ok"), sem("score_ok"), sem("gate_step"))
        w_hi_ok, w_lo_ok, gu_mm, silu_ok, h_ok, h_hi_ok, h_lo_ok, down_mm, y_ok, comb_ok = (
            sem("w_hi_ok"), sem("w_lo_ok"), sem("gu_mm"), sem("silu_ok"), sem("h_ok"), sem("h_hi_ok"),
            sem("h_lo_ok"), sem("down_mm"), sem("y_ok"), sem("comb_ok"))

        block = stack.enter_context(nc.Block())
        LOOP = 2

        def row(p):
            return rows[:, ds(p * D, D)]

        def wait_apart(eng, semaphore, value):
            if not isinstance(value, int):
                value = eng.snap(value)
            eng.wait_ge(x_all_in, 16)
            eng.wait_ge(semaphore, value)

        def split3(pe, out_ap, left_hi, left_lo, right_hi, right_lo, first, last):
            pe.matmul(out_ap, left_hi, right_hi, start=first, stop=False)
            pe.matmul(out_ap, left_hi, right_lo, start=False, stop=False)
            return pe.matmul(out_ap, left_lo, right_hi, start=False, stop=last)

        SPLITS = [("down", 1), ("gu", 0), ("down", 0), ("gu", 1)]

        def expert_part(which, s):
            if which == "gu":
                return gu_raw[s][:, :, :].rearrange("p k n -> p (k n)"), slice(0, KD * I2)
            return dn_raw[s][:, :, :].rearrange("p k n -> p (k n)"), slice(KD * I2, WSZ)

        @block.sync
        def _(sp):
            half = NP // 2
            x_rows = x_pairs.rearrange("n p d -> p n d")
            for k in range(KD):
                sp.dma_start(wq_sb[:, k, :], wq[k * P:(k + 1) * P, :]).then_inc(wqk_in[k], 16)
                sp.dma_start(wk_sb[:, k, :], wk[k * P:(k + 1) * P, :]).then_inc(wqk_in[k], 16)
            sp.dma_start(rows3[:, 0:half, :], x_rows[:, 0:half, :]).then_inc(x_all_in, 16)
            sp.dma_start(rows3[:, half:, :], x_rows[:, half:, :]).then_inc(x_all_in2, 16)

            def load_keys(p, c):
                if not (isinstance(p, int) and p == 0):
                    sp.wait_ge(scored, p * NCH - NCH + c + 1)
                sp.dma_start(keys[:, c, :, 0:width(c)],
                             ctx_t_rows[:, ds(p * (BP * KD), BP * KD), c * CW:c * CW + width(c)]
                             ).then_inc(keys_in[c], 16)

            def load_vals(p, g):
                lo, hi = GROUPS[g]
                slot = lo % RING
                if g == 3:
                    sp.wait_ge(pv_done, p * 4 + 1)
                elif not (isinstance(p, int) and p == 0):
                    sp.wait_ge(pv_done, p * 4)
                for b in range(BP):
                    full = hi - lo if hi < NT else hi - lo - 1
                    start = (p * BP + b) * SK
                    sp.dma_start(vals[:, slot:slot + full, b, :],
                                 ctx_flat[ds(start + lo * P, full * P), :].rearrange("(n p) d -> p n d", p=P)
                                 ).then_inc(vals_in[g], 16)
                    if hi == NT:
                        sp.dma_start(vals[0:TAIL, slot + full, b, :],
                                     ctx_flat[ds(start + (NT - 1) * P, TAIL), :]).then_inc(vals_in[g], 16)

            def load_x(p):
                if not (isinstance(p, int) and p == 0):
                    sp.wait_ge(x1_ok, p)
                sp.dma_start(x_in[:], x_pairs[p]).then_inc(x_in_sem, 16)

            load_keys(0, 0)
            load_keys(0, 1)
            sp.dma_start(wv_raw[:], wv_t.rearrange("(k p) n -> p k n", p=P)).then_inc(wv_in, 16)
            sp.dma_start(wy_raw[:], wy_t.rearrange("(k p) n -> p k n", p=P)).then_inc(wy_in, 16)
            load_keys(0, 2)
            sp.wait_ge(vrep_mm, 1)
            sp.wait_ge(bias_mm, 2)
            load_vals(0, 0)
            load_vals(0, 1)
            sp.wait_ge(cq_ok, NP)
            load_vals(0, 2)
            sp.wait_ge(q_mm, 2 * KD)
            load_keys(0, 3)
            load_x(0)
            load_vals(0, 3)

            def pair_loads(p):
                load_keys(p, 0)
                load_keys(p, 1)
                load_keys(p, 2)
                load_keys(p, 3)
                load_x(p)
                for g in range(4):
                    load_vals(p, g)

            with sp.Fori(1, NP) as p:
                pair_loads(p)

            def load_gu(e, s):
                sp.dma_start(gu_raw[s][:], gu_t[e].rearrange("(k p) n -> p k n", p=P)).then_inc(gu_in[s], 16)

            def load_down(e, s):
                sp.dma_start(dn_raw[s][:], down_t[e].rearrange("(k p) n -> p k n", p=P)).then_inc(dn_in[s], 16)

            sp.wait_ge(pv_done, 4 * NP)
            load_down(0, 0)
            load_down(1, 1)
            sp.wait_ge(vy_mm, NP)
            load_gu(0, 0)
            load_gu(1, 1)
            with sp.Fori(1, E // 2) as e2:
                sp.wait_ge(w_lo_ok, e2 * 4 - 3)
                load_gu(e2 * 2, 0)
                sp.wait_ge(w_lo_ok, e2 * 4 - 2)
                load_down(e2 * 2, 0)
                sp.wait_ge(w_lo_ok, e2 * 4 - 1)
                load_gu(e2 * 2 + 1, 1)
                sp.wait_ge(w_lo_ok, e2 * 4)
                load_down(e2 * 2 + 1, 1)
            for t in range(NP):
                sp.wait_ge(y_ok, (E - 1) * 8 + t + 1)
                sp.dma_start(out_rows[t], rows3[:, t, :]).then_inc(out_done, 16)
            sp.wait_ge(out_done, NP * 16)

        @block.gpsimd
        def _(pool):
            pool.memset(ident[:], 0.0).then_inc(pool_const, 1)
            pool.memset(sel_f[:], 0.0).then_inc(pool_const, 1)
            pool.memset(ex_t[:], 0.0).then_inc(pool_const, 1)
            pool.memset(ew_t[:], 0.0).then_inc(pool_const, 1)
            pool.memset(phi_sel[:], 0.0).then_inc(pool_const, 1)
            pool.memset(small["before"][:], 1.0).then_inc(pool_const, 1)
            pool.memset(small["low_rows"][:], 0.0).then_inc(pool_const, 1)
            pool.wait_ge(pool_const, 7)
            pool.affine_select(out=ident[:], in_=ident[:], compare_op=ALU.not_equal, fill=1.0, base=0,
                               pattern=[[-1, P]], channel_multiplier=1).then_inc(pool_const, 1)
            bf = small["before"][:, :].rearrange("p (e f) -> p e f", e=E)
            pool.affine_select(out=bf, in_=bf, compare_op=ALU.is_gt, fill=0.0, base=0,
                               pattern=[[1, E], [-1, E]], channel_multiplier=0).then_inc(pool_const, 1)
            for low in range(2):
                if low:
                    pool.wait_ge(pool_const, 11)
                for b in range(BP):
                    v = sel_f[:, :, b * A:(b + 1) * A].rearrange("p (g j) a -> p g j a", j=4)
                    pool.affine_select(out=v, in_=v, compare_op=ALU.not_equal, fill=1.0, base=-b - LOW * low,
                                       pattern=[[-2, 2], [-32, 4], [0, A]], channel_multiplier=1
                                       ).then_inc(pool_const, 1)
            v = small["low_rows"][:, :].rearrange("p (j r) -> p j r", j=4)
            pool.affine_select(out=v, in_=v, compare_op=ALU.not_equal, fill=-1.0, base=-LOW,
                               pattern=[[-32, 4], [-1, 4]], channel_multiplier=1).then_inc(pool_const, 1)

            def pair_inputs(p):
                if not (isinstance(p, int) and p == 0):
                    wait_apart(pool, scored, p * NCH)
                pool.tensor_copy(q_cur[:, :, :].rearrange("p k n -> p (k n)"), row(p)).then_inc(q_ready, 1)
                pool.wait_ge(x_in_sem, p * 16 + 16)
                pool.tensor_tensor(x_in[:], x_in[:], bv_b[:], ALU.add).then_inc(xb_ready, 1)

            def plane_half(p):
                pool.wait_ge(qk_ok, p + 1)
                h = SQ // 2
                z = plane[:, h * SQ:].rearrange("p (i j) -> p i j", j=SQ)
                pool.tensor_tensor(z, q2[:, h:SQ].unsqueeze(2).to_broadcast([P, h, SQ]),
                                   k2[:, :].unsqueeze(1).to_broadcast([P, h, SQ]), ALU.add).then_inc(z_pool, 1)

            pool.wait_ge(x_all_in, 16)
            pool.wait_ge(q_ok, KD)
            pool.wait_ge(small_in, 16 * 9)
            pair_inputs(0)
            pool.wait_ge(q_ok, 2 * KD)
            with pool.Fori(1, NP) as p:
                pair_inputs(p)
                plane_half(p - 1)
            plane_half(NP - 1)

            def low_part(which, s, count):
                raw, at = expert_part(which, s)
                pool.wait_ge(w_hi_ok, count)
                pool.tensor_tensor(w_lo[s][:, at], raw, w_hi[s][:, at].bitcast(F32), ALU.subtract).then_inc(w_lo_ok, 1)

            low_part("gu", 0, 1)
            low_part("down", 0, 2)
            low_part("gu", 1, 3)
            with pool.Fori(0, E // 2 - 1) as e2:
                for n, (which, s) in enumerate(SPLITS):
                    low_part(which, s, e2 * 4 + 4 + n)
            low_part("down", 1, 2 * E)

        @block.scalar
        def _(act):
            act.dma_start(small["bq_c"][:], bq).then_inc(bias_in, 16)
            act.dma_start(small["bk_c"][:], bk).then_inc(bias_in, 16)
            act.dma_start(bv_b[:], bv.partition_broadcast(P)).then_inc(small_in, 16)
            act.dma_start(bwe_b[:], we_b.partition_broadcast(P)).then_inc(small_in, 16)
            act.dma_start(tmp[:], wy_b.partition_broadcast(P)).then_inc(small_in, 16)
            act.dma_start(small["gbias"][:], gate_bias.partition_broadcast(P)).then_inc(small_in, 16)
            act.dma_start(wqk_sb[:], wqk_t.rearrange("(k p) n -> p k n", p=P)).then_inc(small_in, 16)
            for b in range(BP):
                act.dma_start(we2[b * A:(b + 1) * A, :], we_t).then_inc(small_in, 16)
                act.dma_start(small["phi_c"][b * A:(b + 1) * A, :], wphi.rearrange("(a n) -> a n", n=1)
                              ).then_inc(small_in, 16)

            def root_of_var(out_ap, var_ap, done):
                act.activation(out_ap, var_ap, ACT.Sqrt, bias=small["eps_ln"][:, 0:1]).then_inc(done, 1)

            act.wait_ge(ln1_stat, NP)
            root_of_var(small["sd1"][:], small["mv1"][:, :].rearrange("p (n t) -> p n t", t=2)[:, :, 1], ln1_sd)
            for m in range(KD):
                act.wait_ge(m_mm, m + 1)
                act.copy(m_hi[:, m, :], ps[:, m, :]).then_inc(m_hi_ok, 1)
            for t in range(NP):
                act.wait_ge(ln1_tr, t + 1)
                act.copy((x1t_hi if t < 4 else x1t_hi2)[:, :, (t % 4) * P:(t % 4 + 1) * P],
                         ps[:, OUT + t % 2, :].rearrange("p (k n) -> p k n", k=KD)).then_inc(ln1_hi, 1)
            act.wait_ge(wv_in, 16)
            act.copy(wv_hi[:], wv_raw[:]).then_inc(wsplit_hi, 1)
            act.wait_ge(wy_in, 16)
            act.copy(wy_hi[:], wy_raw[:]).then_inc(wsplit_hi, 1)
            act.wait_ge(pool_const, POOL_CONSTS)
            act.copy(sel[:], sel_f[:]).then_inc(sel_ok, 1)

            def exp_scores(p):
                if not (isinstance(p, int) and p == 0):
                    act.wait_ge(probs_tr, p * 4)
                    act.wait_ge(rinv_step, p * 2)
                act.wait_ge(ebias_ok, p + 1)
                for c in range(NCH):
                    act.activation(probs[:, c * CW:c * CW + width(c)], ps[:, c, 0:width(c)], ACT.Exp,
                                   bias=small["ebias"][:, 0:1], accum_out=small["sums"][:, c:c + 1]
                                   ).then_inc(exp_done, 1)

            def copy_norm_t(p):
                act.wait_ge(n_tr, p + 1)
                v = ps[:, TRA, :].rearrange("p (k n) -> p k n", k=KD)
                act.copy(nt_f[:], v).then_inc(n_f, 1)
                act.copy(nt_hi[:], v).then_inc(n_hi, 1)

            def copy_vy(p):
                act.wait_ge(vy_mm, p + 1)
                act.copy(vy[:], ps[:, ACC, :]).then_inc(vy_ok, 1)

            def copy_probs_t(p):
                for g in (1, 3):
                    lo, hi = GROUPS[g]
                    full = hi - lo if hi < NT else hi - lo - 1
                    act.wait_ge(probs_tr, p * 4 + g + 1)
                    ins = act.copy(probs_t[:, lo:lo + full, :],
                                   ps[:, TRB, 0:full * P].rearrange("p (k n) -> p k n", n=P))
                    if hi == NT:
                        ins = act.copy(probs_t[0:TAIL, NT - 1, :], ps[0:TAIL, TRB, full * P:(full + 1) * P])
                    ins.then_inc(pt_act, 1)

            def roots(p):
                for h in range(2):
                    act.wait_ge(relu_ok, p * 2 + h + 1)
                    v = plane[:, h * 2048:(h + 1) * 2048]
                    act.activation(v, v, ACT.Sqrt, bias=small["eps_rho"][:, 0:1]).then_inc(root_ok, 1)

            def copy_o_t(p):
                act.wait_ge(o_tr, p + 1)
                act.copy(nt_hi[:], ps[:, TRA, :].rearrange("p (k n) -> p k n", k=KD)).then_inc(o_hi, 1)

            def exp_pairwise(p):
                act.wait_ge(s16_sub, p + 1)
                act.activation(ex[:], ex[:], ACT.Exp).then_inc(s16_exp, 1)
                act.wait_ge(s16_exp, p + 1)
                act.copy(ex_hi[:], ex[:]).then_inc(ex_hi_ok, 1)

            def root2(p):
                act.wait_ge(ln2_stat, p * 2 + 2)
                root_of_var(small["sd2"][:], small["mv2"][:, 1:2], ln2_sd)

            def both(t, cross, pairwise):
                if pairwise:
                    copy_norm_t(t - 1)
                if cross:
                    exp_scores(t)
                if cross:
                    copy_probs_t(t)
                if pairwise:
                    roots(t - 1)
                    copy_vy(t - 1)
                    exp_pairwise(t - 1)
                if cross:
                    copy_o_t(t)
                    root2(t)

            both(0, True, False)
            both(1, True, True)
            with act.Fori(LOOP, NP) as t:
                both(t, True, True)
            both(NP, False, True)

            def high_part(which, s, arrived, fills):
                raw, at = expert_part(which, s)
                act.wait_ge(arrived[s], fills * 16)
                act.copy(w_hi[s][:, at], raw).then_inc(w_hi_ok, 1)

            act.wait_ge(gate_zero, 1)
            act.dma_start(gate_sb[:, :, 0:E], gate_t.rearrange("(k p) n -> p k n", p=P)).then_inc(gate_in, 16)
            act.wait_ge(ln3_stat, NP)
            root_of_var(small["sd3"][:], small["mv3"][:, :].rearrange("p (n t) -> p n t", t=2)[:, :, 1], ln3_sd)
            for t in range(NP):
                act.wait_ge(x3_tr, t + 1)
                act.copy(x3_hi[:, :, t * P:(t + 1) * P],
                         ps[:, TRA + t % 2, :].rearrange("p (k n) -> p k n", k=KD)).then_inc(x3_hi_ok, 1)
            act.wait_ge(gate_in, 16)
            act.copy(gate_hi[:], gate_sb[:]).then_inc(gate_split_hi, 1)
            high_part("gu", 0, gu_in, 1)
            high_part("down", 0, dn_in, 1)
            high_part("gu", 1, gu_in, 1)
            for h in range(2):
                act.wait_ge(logit_mm, h + 1)
                act.copy(logit_t[:, h * 512:(h + 1) * 512], ps[0:E, OUT + h, :]).then_inc(logit_ok, 1)
            act.wait_ge(logits_ok, 1)
            act.activation(small["score"][:], small["logits"][:], ACT.Sigmoid).then_inc(score_ok, 1)

            def silu_step(s, u):
                for n in range(2):
                    act.wait_ge(gu_mm, s * 2 + n + 1)
                    if not (isinstance(s, int) and s == 0):
                        act.wait_ge(h_ok, s * 2 - 1 + n)
                    act.activation(silu_sb[:, n, :], ps[:, 2 * n, :], ACT.Silu).then_inc(silu_ok, 1)
                for n in range(2):
                    act.wait_ge(h_ok, s * 2 + n + 1)
                    if not (isinstance(s, int) and s < 2):
                        act.wait_ge(down_mm, s * 4 - 4)
                    act.copy(h_hi[u][:, n, :], h_sb[:, n, :]).then_inc(h_hi_ok, 1)

            def expert_pair(e2, last):
                silu_step(e2 * 4, 0)
                silu_step(e2 * 4 + 1, 1)
                if not (isinstance(e2, int) and e2 == 0):
                    act.wait_ge(down_mm, e2 * 16)
                high_part("down", 1, dn_in, e2 + 1)
                if not last:
                    high_part("gu", 0, gu_in, e2 + 2)
                silu_step(e2 * 4 + 2, 0)
                silu_step(e2 * 4 + 3, 1)
                if not last:
                    act.wait_ge(down_mm, e2 * 16 + 8)
                    high_part("down", 0, dn_in, e2 + 2)
                    high_part("gu", 1, gu_in, e2 + 2)

            expert_pair(0, False)
            with act.Fori(1, E // 2 - 1) as e2:
                expert_pair(e2, False)
            expert_pair(E // 2 - 1, True)

        @block.vector
        def _(dve):
            sm = small
            dve.memset(sm["ones"][:], 1.0).then_inc(vec_const, 1)
            dve.memset(sm["eps_ln"][:], LN_EPS).then_inc(vec_const, 1)
            dve.memset(sm["eps_rho"][:], EPS_RHO).then_inc(vec_const, 1)
            dve.memset(bk_rep[:], 1.0).then_inc(vec_const, 1)
            dve.memset(bq_rep[:], 1.0).then_inc(vec_const, 1)
            dve.wait_ge(vec_const, 5)
            dve.wait_ge(bias_in, 32)
            for k in range(KD):
                dve.tensor_scalar(bq_rep[:, k, :], bq_rep[:, k, :], sm["bq_c"][:, k:k + 1], None, ALU.mult)
                ins = dve.tensor_scalar(bk_rep[:, k, :], bk_rep[:, k, :], sm["bk_c"][:, k:k + 1], None, ALU.mult)
            ins.then_inc(bk_rep_ok, 1)
            for t in range(NP):
                if t == 0:
                    dve.wait_ge(x_all_in, 16)
                elif t == NP // 2:
                    dve.wait_ge(x_all_in2, 16)
                dve.bn_stats(sm["st1"][:, 6 * t:6 * t + 6], rows3[:, t, :]).then_inc(ln1_rs, 1)
            for t in range(NP):
                dve.wait_ge(ln1_rs, t + 1)
                dve.bn_aggr(sm["mv1"][:, 2 * t:2 * t + 2], sm["st1"][:, 6 * t:6 * t + 6]).then_inc(ln1_stat, 1)
            dve.wait_ge(ln1_sd, 1)
            dve.reciprocal(sm["rs1"][:], sm["sd1"][:]).then_inc(ln1_rs, 1)
            dve.wait_ge(ln1_rs, NP + 1)
            for t in range(NP):
                dve.tensor_scalar(rows3[:, t, :], rows3[:, t, :], sm["mv1"][:, 2 * t:2 * t + 1],
                                  sm["rs1"][:, t:t + 1], ALU.subtract, ALU.mult).then_inc(ln1_ok, 1)
            for m in range(KD):
                dve.wait_ge(m_hi_ok, m + 1)
                dve.tensor_tensor(m_lo[:, m, :], ps[:, m, :], m_hi[:, m, :].bitcast(F32), ALU.subtract
                                  ).then_inc(m_lo_ok, 1)
            for t in range(NP):
                if t == 1:
                    dve.wait_ge(vrep_mm, 1)
                    dve.tensor_copy(v_rep[:], ps[:, TRA, :]).then_inc(bias_ok, 1)
                elif t == 4:
                    dve.wait_ge(bias_mm, 1)
                    dve.tensor_copy(sm["kbias"][:], ps[:, TRB, :].rearrange("p (m n) -> p m n", n=P)[:, :, 0]
                                    ).then_inc(bias_ok, 1)
                elif t == 5:
                    dve.wait_ge(bias_mm, 2)
                    dve.tensor_copy(sm["c0"][:], ps[:, TRA, 0:1]).then_inc(bias_ok, 1)
                at = slice((t % 4) * P, (t % 4 + 1) * P)
                hi, lo = (x1t_hi, x1t_lo) if t < 4 else (x1t_hi2, x1t_lo2)
                dve.wait_ge(ln1_hi, t + 1)
                dve.tensor_tensor(lo[:, :, at], ps[:, OUT + t % 2, :].rearrange("p (k n) -> p k n", k=KD),
                                  hi[:, :, at].bitcast(F32), ALU.subtract).then_inc(ln1_lo, 1)
            dve.wait_ge(ln1_ok, NP)
            dve.wait_ge(bias_ok, 3)
            for t in range(NP):
                dve.tensor_tensor_reduce(out=ex[:], in0=rows3[:, t, :],
                                         in1=v_rep[:], scale=1.0, scalar=0.0, op0=ALU.mult, op1=ALU.add,
                                         accum_out=sm["cq"][:, t:t + 1]).then_inc(cq_ok, 1)
                dve.wait_ge(cq_ok, t + 1)
            dve.tensor_scalar(sm["cq"][:], sm["cq"][:], sm["c0"][:, 0:1], None, ALU.add).then_inc(cq_ok, 1)
            for h in range(2):
                for m in range(KD):
                    dve.wait_ge(q_mm, h * KD + m + 1)
                    dve.tensor_scalar(rows3[:, 4 * h:4 * h + 4, m * P:(m + 1) * P],
                                      ps[:, 4 * h + m, :].rearrange("p (t n) -> p t n", t=4), sm["kbias"][:, m:m + 1], None,
                                      ALU.add).then_inc(q_ok, 1)
            dve.wait_ge(wsplit_hi, 1)
            dve.tensor_tensor(wv_lo[:], wv_raw[:], wv_hi[:].bitcast(F32), ALU.subtract).then_inc(wsplit_lo, 1)
            dve.wait_ge(wsplit_hi, 2)
            dve.tensor_tensor(wy_lo[:], wy_raw[:], wy_hi[:].bitcast(F32), ALU.subtract).then_inc(wsplit_lo, 1)
            dve.wait_ge(small_in, 16 * 9)
            dve.wait_ge(pool_const, POOL_CONSTS)
            dve.reduce_sum(sm["minus_low"][:], sm["low_rows"][:], AX.X).then_inc(low_rows_ok, 1)
            for b in range(BP):
                for g in range(2):
                    for at in (g * 2 + b, LOW + g * 2 + b):
                        dve.tensor_copy(phi_sel[b * A:(b + 1) * A, g, at:at + 1], sm["phi_c"][b * A:(b + 1) * A, :]
                                        ).then_inc(phi_ok, 1)
            dve.tensor_tensor(bwe_b[:], bwe_b[:], tmp[:], ALU.add).then_inc(bwe_ok, 1)
            dve.wait_ge(cq_ok, NP + 1)
            dve.wait_ge(low_rows_ok, 1)

            def chunk_max(p, c):
                dve.wait_ge(scored, p * NCH + c + 1)
                dve.reduce_max(sm["mx"][:, c:c + 1], ps[:, c, 0:width(c)], AX.X).then_inc(max_step, 1)

            def row_max(p):
                dve.wait_ge(max_step, p * 6 + 4)
                dve.reduce_max(sm["mx1"][:], sm["mx"][:], AX.X).then_inc(max_step, 1)
                dve.wait_ge(max_step, p * 6 + 5)
                dve.tensor_tensor(sm["smax"][:], sm["mx1"][:], sm["cq"][:, ds(p, 1)], ALU.add).then_inc(max_step, 1)
                dve.wait_ge(max_step, p * 6 + 6)
                if not (isinstance(p, int) and p == 0):
                    dve.wait_ge(exp_done, p * NCH)
                dve.tensor_tensor(sm["ebias"][:], sm["cq"][:, ds(p, 1)], sm["smax"][:], ALU.subtract
                                  ).then_inc(ebias_ok, 1)

            def finish_pair(p):
                dve.wait_ge(den_mm, p + 1)
                dve.tensor_copy(sm["den"][:], ps[:, TRB, 0:1]).then_inc(den_ok, 1)
                dve.wait_ge(den_ok, p * 2 + 1)
                dve.tensor_scalar(sm["den1"][:], sm["den"][:], EPS_DEN, None, ALU.add).then_inc(den_ok, 1)
                dve.wait_ge(den_ok, p * 2 + 2)
                dve.reciprocal(sm["rden"][:], sm["den1"][:]).then_inc(rden_ok, 1)
                dve.wait_ge(part_mm, p + 1)
                dve.scalar_tensor_tensor(out=tmp[:], in0=bwe_b[:], scalar=sm["den"][:, 0:1], in1=ps[:, OUT, :],
                                         op0=ALU.mult, op1=ALU.add).then_inc(tmp_ok, 1)
                dve.wait_ge(rden_ok, p + 1)
                dve.wait_ge(tmp_ok, p + 1)
                dve.scalar_tensor_tensor(out=row(p), in0=tmp[:], scalar=sm["rden"][:, 0:1], in1=row(p),
                                         op0=ALU.mult, op1=ALU.add).then_inc(x2_ok, 1)
                dve.wait_ge(x2_ok, p + 1)
                dve.wait_ge(x_all_in, 16)
                dve.bn_stats(sm["st3"][:, ds(p * 6, 6)], row(p)).then_inc(st3_ok, 1)

            def low_norm_t(p):
                dve.wait_ge(n_hi, p + 1)
                dve.tensor_tensor(nt_lo[:], ps[:, TRA, :].rearrange("p (k n) -> p k n", k=KD),
                                  nt_hi[:].bitcast(F32), ALU.subtract).then_inc(n_lo, 1)

            def copy_qk(p):
                dve.wait_ge(qk_mm, p + 1)
                if not (isinstance(p, int) and p == 0):
                    dve.wait_ge(z_pool, p)
                for b in range(BP):
                    dve.tensor_copy(q2[b * A:(b + 1) * A, :], ps[0:A, TRB, b * SQ:(b + 1) * SQ])
                    ins = dve.tensor_copy(k2[b * A:(b + 1) * A, :], ps[A:2 * A, TRB, b * SQ:(b + 1) * SQ])
                ins.then_inc(qk_ok, 1)

            def plane_half(p):
                dve.wait_ge(qk_ok, p + 1)
                h = SQ // 2
                z = plane[:, 0:h * SQ].rearrange("p (i j) -> p i j", j=SQ)
                dve.tensor_tensor(z, q2[:, 0:h].unsqueeze(2).to_broadcast([P, h, SQ]),
                                  k2[:, :].unsqueeze(1).to_broadcast([P, h, SQ]), ALU.add).then_inc(z_dve, 1)

            def relu_half(p, h):
                dve.wait_ge((z_dve, z_pool)[h], p + 1)
                v = plane[:, h * 2048:(h + 1) * 2048]
                dve.tensor_scalar(v, v, 0.0, None, ALU.max).then_inc(relu_ok, 1)

            def copy_probs_t(p):
                for g in (0, 2):
                    lo, hi = GROUPS[g]
                    dve.wait_ge(probs_tr, p * 4 + g + 1)
                    dve.tensor_copy(probs_t[:, lo:hi, :],
                                    ps[:, TRA, 0:(hi - lo) * P].rearrange("p (k n) -> p k n", n=P)).then_inc(pt_dve, 1)

            def normalise(p):
                dve.wait_ge(exp_done, p * NCH + NCH)
                dve.reduce_sum(sm["ssum"][:], sm["sums"][:], AX.X).then_inc(rinv_step, 1)
                dve.wait_ge(rinv_step, p * 2 + 1)
                dve.reciprocal(sm["rinv"][:], sm["ssum"][:]).then_inc(rinv_step, 1)
                dve.wait_ge(rinv_step, p * 2 + 2)
                dve.wait_ge(pv_done, p * 4 + 4)
                dve.tensor_scalar(norm[:], ps[:, OUT, :], sm["rinv"][:, 0:1], None, ALU.mult).then_inc(attended_ok, 1)

            def low_o_t(p):
                dve.wait_ge(o_hi, p + 1)
                dve.tensor_tensor(nt_lo[:], ps[:, TRA, :].rearrange("p (k n) -> p k n", k=KD),
                                  nt_hi[:].bitcast(F32), ALU.subtract).then_inc(o_lo, 1)

            def pairwise_softmax(p):
                dve.wait_ge(s16_mm, p + 1)
                v = ps[:, TRB, :].rearrange("p (i j) -> p i j", j=SQ)
                dve.reduce_max(sm["mx16"][:], v, AX.X).then_inc(s16_max, 1)
                dve.wait_ge(s16_max, p + 1)
                dve.tensor_tensor(ex[:, :].rearrange("p (i j) -> p i j", j=SQ), v,
                                  sm["mx16"][:, :].unsqueeze(2).to_broadcast([P, 8, SQ]), ALU.subtract
                                  ).then_inc(s16_sub, 1)

            def parts_of_ex(p):
                dve.wait_ge(ex_hi_ok, p + 1)
                dve.scalar_tensor_tensor(out=ex_parts[:], in0=ex_hi[:].bitcast(F32), scalar=sm["minus_low"][:, 0:1],
                                         in1=ex[:], op0=ALU.mult, op1=ALU.add).then_inc(ex_parts_ok, 1)

            def add_x(p):
                dve.wait_ge(vproj, p + 1)
                dve.wait_ge(xb_ready, p + 1)
                dve.wait_ge(q_ready, p + 1)
                dve.tensor_tensor(row(p), ps[:, ACC, :], x_in[:], ALU.add).then_inc(x1_ok, 1)

            def stats2(p):
                wait_apart(dve, x1_ok, p + 1)
                dve.bn_stats(sm["st2"][:], row(p)).then_inc(ln2_stat, 1)
                wait_apart(dve, ln2_stat, p * 2 + 1)
                dve.bn_aggr(sm["mv2"][:], sm["st2"][:]).then_inc(ln2_stat, 1)

            def norm2(p):
                dve.wait_ge(ln2_sd, p + 1)
                dve.reciprocal(sm["rs2"][:], sm["sd2"][:]).then_inc(ln2_rs, 1)
                dve.wait_ge(ln2_rs, p + 1)
                dve.tensor_scalar(norm[:], row(p), sm["mv2"][:, 0:1], sm["rs2"][:, 0:1], ALU.subtract, ALU.mult
                                  ).then_inc(ln2_ok, 1)

            def gather_ex_t(p):
                dve.wait_ge(ex_tr, p + 1)
                for b in range(BP):
                    for par in range(2):
                        dst = ex_t[b * SQ:(b + 1) * SQ, b * SQ:(b + 1) * SQ].rearrange(
                            "p (g j m s) -> p g j m s", g=2, j=4, m=4)[:, :, :, :, par]
                        src = ps[par * SQ:(par + 1) * SQ, TRB, :].rearrange(
                            "p (m j r) -> p r j m", m=4, j=4)[:, b:b + 3:2, :, :]
                        ins = dve.tensor_copy(dst, src)
                ins.then_inc(ex_t_ok, 1)

            def products(p, lo, hi):
                for c in range(lo, hi):
                    dve.wait_ge(spread, p * NC8 + c + 1)
                    v = plane[:, c * 512:(c + 1) * 512]
                    dve.scalar_tensor_tensor(out=v, in0=v, scalar=-ROOT_EPS_RHO, in1=ps[:, c % 4, :],
                                             op0=ALU.add, op1=ALU.mult).then_inc(prod, 1)

            def sum_products(p):
                dve.wait_ge(prod, p * NC8 + NC8)
                dve.reduce_sum(ew[:], plane[:, :].rearrange("p (i j) -> p i j", j=SQ), AX.X).then_inc(ew_red, 1)
                dve.wait_ge(ew_red, p + 1)
                for b in range(BP):
                    ins = dve.tensor_copy(ew_t[b * A:(b + 1) * A, b * SQ:(b + 1) * SQ], ew[b * A:(b + 1) * A, :])
                ins.then_inc(ew_ok, 1)

            def both(t, cross, pairwise, ending):
                if cross:
                    chunk_max(t, 0)
                    chunk_max(t, 1)
                if cross:
                    chunk_max(t, 2)
                if ending:
                    finish_pair(t - 2)
                if pairwise:
                    low_norm_t(t - 1)
                if cross:
                    chunk_max(t, 3)
                    row_max(t)
                if pairwise:
                    copy_qk(t - 1)
                    plane_half(t - 1)
                if cross:
                    copy_probs_t(t)
                if pairwise:
                    relu_half(t - 1, 0)
                    relu_half(t - 1, 1)
                    pairwise_softmax(t - 1)
                    parts_of_ex(t - 1)
                    gather_ex_t(t - 1)
                    products(t - 1, 0, 4)
                if cross:
                    normalise(t)
                if pairwise:
                    products(t - 1, 4, 6)
                if cross:
                    low_o_t(t)
                if pairwise:
                    products(t - 1, 6, NC8)
                if cross:
                    add_x(t)
                    stats2(t)
                    norm2(t)
                if pairwise:
                    sum_products(t - 1)

            both(0, True, False, False)
            both(1, True, True, False)
            with dve.Fori(LOOP, NP) as t:
                both(t, True, True, True)
            both(NP, False, True, True)
            finish_pair(NP - 1)

            dve.wait_ge(probs_tr, NP * 4)
            dve.memset(gate_sb[:], 0.0).then_inc(gate_zero, 1)
            dve.wait_ge(st3_ok, NP)
            for t in range(NP):
                dve.bn_aggr(sm["mv3"][:, 2 * t:2 * t + 2], sm["st3"][:, 6 * t:6 * t + 6]).then_inc(ln3_stat, 1)
            dve.wait_ge(ln3_sd, 1)
            dve.reciprocal(sm["rs3"][:], sm["sd3"][:]).then_inc(ln3_rs, 1)
            dve.wait_ge(ln3_rs, 1)

            def apply3(t):
                if t >= 2:
                    dve.wait_ge(x3_tr, t - 1)
                dve.tensor_scalar(n3[t % 2][:], rows3[:, t, :], sm["mv3"][:, 2 * t:2 * t + 1], sm["rs3"][:, t:t + 1],
                                  ALU.subtract, ALU.mult).then_inc(ln3_ok, 1)

            apply3(0)
            for t in range(NP):
                if t + 1 < NP:
                    apply3(t + 1)
                dve.wait_ge(x3_hi_ok, t + 1)
                dve.tensor_tensor(x3_lo[:, :, t * P:(t + 1) * P],
                                  ps[:, TRA + t % 2, :].rearrange("p (k n) -> p k n", k=KD),
                                  x3_hi[:, :, t * P:(t + 1) * P].bitcast(F32), ALU.subtract).then_inc(x3_lo_ok, 1)
            dve.wait_ge(gate_split_hi, 1)
            dve.tensor_tensor(gate_lo[:], gate_sb[:], gate_hi[:].bitcast(F32), ALU.subtract).then_inc(gate_split_lo, 1)
            dve.wait_ge(logit_tr, 1)
            dve.tensor_copy(sm["logits"][:], ps[:, TRA, 0:NP * E]).then_inc(logits_ok, 1)
            dve.wait_ge(score_ok, 1)
            steps = [0]

            def link(ins):
                ins.then_inc(gate_step, 1)
                steps[0] += 1
                dve.wait_ge(gate_step, steps[0])

            G = E // 2

            def v3(name, n):
                return sm[name][:, :].rearrange("p (t e) -> p t e", e=n)

            def beaten(out_name, in_name, n):
                mine = v3(in_name, n).unsqueeze(3).to_broadcast([P, NP, n, n])
                other = v3(in_name, n).unsqueeze(2).to_broadcast([P, NP, n, n])
                first = sm["before"][:, :].rearrange("p (e f) -> p e f", e=E)[:, 0:n, 0:n].unsqueeze(1).to_broadcast(
                    [P, NP, n, n])
                link(dve.tensor_tensor(tie[:, :, 0:n, 0:n], mine, other, ALU.is_equal))
                for q in range(NP):
                    ins = dve.tensor_tensor(tie[:, q, 0:n, 0:n], tie[:, q, 0:n, 0:n], first[:, q], ALU.mult)
                link(ins)
                link(dve.tensor_tensor(beat[:, :, 0:n, 0:n], other, mine, ALU.is_gt))
                link(dve.tensor_tensor(beat[:, :, 0:n, 0:n], beat[:, :, 0:n, 0:n], tie[:, :, 0:n, 0:n], ALU.add))
                link(dve.reduce_sum(v3(out_name, n), beat[:, :, 0:n, 0:n], AX.X))

            link(dve.tensor_tensor(v3("choice", E), v3("score", E),
                                   sm["gbias"][:, :].unsqueeze(1).to_broadcast([P, NP, E]), ALU.add))
            pairs_of = sm["choice"][:, :].rearrange("p (t g e) -> p t g e", g=G, e=2)
            link(dve.tensor_tensor(v3("grp", G), pairs_of[:, :, :, 0], pairs_of[:, :, :, 1], ALU.add))
            beaten("grank", "grp", G)
            link(dve.tensor_scalar(sm["gmask"][:], sm["grank"][:], 2.0, None, ALU.is_lt))
            link(dve.tensor_tensor(sm["kept"][:, :].rearrange("p (t g e) -> p (t g) e", g=G, e=2),
                                   sm["choice"][:, :].rearrange("p (t g e) -> p (t g) e", g=G, e=2),
                                   sm["gmask"][:, :].unsqueeze(2).to_broadcast([P, NP * G, 2]), ALU.mult))
            link(dve.tensor_scalar(sm["kept"][:], sm["kept"][:], 0.0, None, ALU.add))
            beaten("rank", "kept", E)
            link(dve.tensor_scalar(sm["rank"][:], sm["rank"][:], 2.0, None, ALU.is_lt))
            link(dve.tensor_tensor(sm["wsel"][:], sm["score"][:], sm["rank"][:], ALU.mult))
            link(dve.reduce_sum(sm["wsum"][:], v3("wsel", E), AX.X))
            link(dve.tensor_scalar(sm["wsum"][:], sm["wsum"][:], EPS_TOPK, None, ALU.add))
            link(dve.reciprocal(sm["winv"][:], sm["wsum"][:]))
            link(dve.tensor_tensor(sm["comb"][:, :].rearrange("p (e t) -> p t e", e=E), v3("wsel", E),
                                   sm["winv"][:, :].unsqueeze(2).to_broadcast([P, NP, E]), ALU.mult))

            comb_e = [sm["comb_e0"], sm["comb_e1"]]

            def h_step(s, u):
                for n in range(2):
                    dve.wait_ge(silu_ok, s * 2 + n + 1)
                    if not (isinstance(s, int) and s == 0):
                        dve.wait_ge(h_lo_ok, s * 2 - 1 + n)
                    dve.tensor_tensor(h_sb[:, n, :], silu_sb[:, n, :], ps[:, 2 * n + 1, :], ALU.mult).then_inc(h_ok, 1)
                for n in range(2):
                    dve.wait_ge(h_hi_ok, s * 2 + n + 1)
                    dve.tensor_tensor(h_lo[u][:, n, :], h_sb[:, n, :], h_hi[u][:, n, :].bitcast(F32), ALU.subtract
                                      ).then_inc(h_lo_ok, 1)

            def add_step(s, h, slot):
                for j in range(4):
                    r = rows3[:, h * 4 + j, :]
                    dve.wait_ge(down_mm, s * 4 + j + 1)
                    dve.scalar_tensor_tensor(out=r, in0=ps[:, 4 + j, :], scalar=comb_e[slot][:, h * 4 + j:h * 4 + j + 1],
                                             in1=r, op0=ALU.mult, op1=ALU.add).then_inc(y_ok, 1)

            def four(e2, last):
                if not (isinstance(e2, int) and e2 == 0):
                    dve.wait_ge(y_ok, e2 * 16)
                for s in range(2):
                    dve.tensor_copy(comb_e[s][:], sm["comb"][:, ds(e2 * (2 * NP) + s * NP, NP)]).then_inc(comb_ok, 1)
                dve.wait_ge(comb_ok, e2 * 2 + 2)
                for u in range(4):
                    if not (last and u == 3):
                        h_step(e2 * 4 + u + 1, (u + 1) % 2)
                    add_step(e2 * 4 + u, u % 2, u // 2)

            h_step(0, 0)
            four(0, False)
            with dve.Fori(1, E // 2 - 1) as e2:
                four(e2, False)
            four(E // 2 - 1, True)

        @block.tensor
        def _(pe):
            for k in range(KD):
                pe.wait_ge(wqk_in[k], 32)
                for m in range(KD):
                    ins = pe.matmul(ps[:, m, :], wq_sb[:, k, m * P:(m + 1) * P], wk_sb[:, k, :], start=(k == 0),
                                    stop=(k == KD - 1))
                    if k == KD - 1:
                        ins.then_inc(m_mm, 1)

            def turn_rows(t):
                pe.wait_ge(ln1_ok, t + 1)
                if t >= 2:
                    pe.wait_ge(ln1_lo, t - 1)
                for k in range(KD):
                    ins = pe.transpose(ps[:, OUT + t % 2, k * P:(k + 1) * P], rows3[:, t, k * P:(k + 1) * P], ident[:])
                ins.then_inc(ln1_tr, 1)

            def wk_bias(m):
                for k in range(KD):
                    ins = pe.matmul(ps[:, TRB, m * P:(m + 1) * P], wk_sb[:, k, m * P:(m + 1) * P], bq_rep[:, k, :],
                                    start=(k == 0), stop=(k == KD - 1))
                if m == KD - 1:
                    ins.then_inc(bias_mm, 1)

            pe.wait_ge(bk_rep_ok, 1)
            pe.wait_ge(pool_const, POOL_CONSTS)
            turn_rows(0)
            for k in range(KD):
                ins = pe.matmul(ps[:, TRA, :], bk_rep[:, k, :], wq_sb[:, k, :], start=(k == 0), stop=(k == KD - 1))
            ins.then_inc(vrep_mm, 1)
            turn_rows(1)
            wk_bias(0)
            turn_rows(2)
            wk_bias(1)
            turn_rows(3)
            wk_bias(2)
            turn_rows(4)
            wk_bias(3)
            turn_rows(5)
            pe.wait_ge(bias_ok, 1)
            for k in range(KD):
                ins = pe.matmul(ps[:, TRA, 0:P], bk_rep[:, k, :], bq_rep[:, k, :], start=(k == 0), stop=(k == KD - 1))
            ins.then_inc(bias_mm, 1)
            turn_rows(6)
            turn_rows(7)
            pe.wait_ge(m_lo_ok, KD)
            for h, (hi, lo) in enumerate(((x1t_hi, x1t_lo), (x1t_hi2, x1t_lo2))):
                pe.wait_ge(ln1_lo, 4 * h + 4)
                if h:
                    pe.wait_ge(bias_ok, 3)
                for m in range(KD):
                    for k in range(KD):
                        ins = split3(pe, ps[:, 4 * h + m, :], m_hi[:, k, m * P:(m + 1) * P],
                                     m_lo[:, k, m * P:(m + 1) * P], hi[:, k, :], lo[:, k, :], k == 0, k == KD - 1)
                    ins.then_inc(q_mm, 1)

            def scores(p, chunks):
                if 0 in chunks:
                    pe.wait_ge(q_ready, p + 1)
                for c in chunks:
                    pe.wait_ge(keys_in[c], p * 16 + 16)
                    if isinstance(p, int):
                        if p == 0:
                            pe.wait_ge(q_ok, c + 1)
                        elif p == 1:
                            pe.wait_ge(exp_done, c + 1)
                    else:
                        pe.wait_ge(prod, p * NC8 - 2 * NC8 + c + 5)
                    for k in range(KD):
                        for b in range(BP):
                            ins = pe.matmul(ps[b * SQ:(b + 1) * SQ, c, 0:width(c)],
                                            q_cur[:, k, b * SQ:(b + 1) * SQ], keys[:, c, b * KD + k, 0:width(c)],
                                            start=(k == 0), stop=(k == KD - 1))
                    ins.then_inc(scored, 1)

            def first_part(p):
                pe.wait_ge(ex_t_ok, p + 1)
                pe.matmul(ps[:, TRB, 0:2], ex_t[:], small["ones"][:], start=True, stop=True).then_inc(den_mm, 1)
                if not (isinstance(p, int) and p == NP - 1):
                    pe.wait_ge(attended_ok, p + 2)
                pe.wait_ge(vy_ok, p + 1)
                pe.matmul(ps[:, OUT, :], ex_t[:], vy[:], start=True, stop=False)

            def second_part(p):
                pe.wait_ge(ew_ok, p + 1)
                pe.matmul(ps[:, OUT, :], ew_t[:], we2[:], start=False, stop=True).then_inc(part_mm, 1)

            def norm_t(p):
                pe.wait_ge(ln2_ok, p + 1)
                pe.wait_ge(o_lo, p + 1)
                for k in range(KD):
                    ins = pe.transpose(ps[:, TRA, k * P:(k + 1) * P], norm[:, k * P:(k + 1) * P], ident[:])
                ins.then_inc(n_tr, 1)

            def pairwise_qk(p):
                pe.wait_ge(n_f, p + 1)
                if not (isinstance(p, int) and p == 0):
                    pe.wait_ge(den_ok, p * 2)
                else:
                    pe.wait_ge(pt_act, 2)
                for k in range(KD):
                    ins = pe.matmul(ps[:, TRB, 0:P], wqk_sb[:, k, :], nt_f[:, k, :], start=(k == 0),
                                    stop=(k == KD - 1))
                ins.then_inc(qk_mm, 1)

            def values_y(p):
                pe.wait_ge(n_lo, p + 1)
                pe.wait_ge(x1_ok, p + 1)
                if isinstance(p, int) and p == 0:
                    pe.wait_ge(wsplit_lo, 2)
                for k in range(KD):
                    ins = split3(pe, ps[:, ACC, :], nt_hi[:, k, :], nt_lo[:, k, :], wy_hi[:, k, :], wy_lo[:, k, :],
                                 k == 0, k == KD - 1)
                ins.then_inc(vy_mm, 1)

            def turn_probs(p, pairwise):
                for g, (lo, hi) in enumerate(GROUPS):
                    if g < 3:
                        pe.wait_ge(exp_done, p * NCH + -(-hi * P // CW))
                    if g == 0 and not pairwise:
                        pe.wait_ge(q_ok, 2 * KD)
                    if g == 0 and pairwise:
                        pe.wait_ge(n_lo, p)
                    if g == 1 and pairwise:
                        pe.wait_ge(qk_ok, p)
                    if g == 2:
                        pe.wait_ge(pt_dve, p * 2 + 1)
                    if g == 3:
                        pe.wait_ge(pt_act, p * 2 + 1)
                    for n in range(lo, hi):
                        w = P if n < NT - 1 else TAIL
                        ins = pe.transpose(ps[0:w, TRA + g % 2, (n - lo) * P:(n - lo + 1) * P],
                                           probs[:, n * P:n * P + w], ident[:])
                    ins.then_inc(probs_tr, 1)

            def attend(p, groups):
                for g in groups:
                    lo, hi = GROUPS[g]
                    if g % 2 == 0:
                        pe.wait_ge(pt_dve, p * 2 + g // 2 + 1)
                    else:
                        pe.wait_ge(pt_act, p * 2 + g // 2 + 1)
                    if g == 0 and not (isinstance(p, int) and p < 2):
                        pe.wait_ge(tmp_ok, p - 1)
                    pe.wait_ge(vals_in[g], (p + 1) * (64 if hi == NT else 32))
                    for n in range(lo, hi):
                        w = P if n < NT - 1 else TAIL
                        for b in range(BP):
                            ins = pe.matmul(ps[b * SQ:(b + 1) * SQ, OUT, :], probs_t[0:w, n, b * SQ:(b + 1) * SQ],
                                            vals[0:w, n % RING, b, :], start=(n == 0), stop=(n == NT - 1))
                    ins.then_inc(pv_done, 1)

            def turn_attended(p):
                pe.wait_ge(attended_ok, p + 1)
                for k in range(KD):
                    ins = pe.transpose(ps[:, TRA, k * P:(k + 1) * P], norm[:, k * P:(k + 1) * P], ident[:])
                ins.then_inc(o_tr, 1)

            def pairwise_scores(p):
                if isinstance(p, int) and p == 0:
                    pe.wait_ge(phi_ok, 8)
                if not (isinstance(p, int) and p == NP - 1):
                    pe.wait_ge(pt_act, p * 2 + 4)
                for c in range(NC8):
                    if c % 4 == 0:
                        pe.wait_ge(root_ok, p * 2 + c // 4 + 1)
                    j = c % 4
                    ins = pe.matmul(ps[32 * j:32 * j + 32, TRB, :], phi_sel[:, c // 4, :],
                                    plane[:, c * 512:(c + 1) * 512], start=(c < 4), stop=(c >= 4))
                ins.then_inc(s16_mm, 1)

            def project(p):
                pe.wait_ge(o_lo, p + 1)
                if isinstance(p, int) and p == 0:
                    pe.wait_ge(wsplit_lo, 1)
                else:
                    pe.wait_ge(vy_ok, p)
                for k in range(KD):
                    ins = split3(pe, ps[:, ACC, :], nt_hi[:, k, :], nt_lo[:, k, :], wv_hi[:, k, :], wv_lo[:, k, :],
                                 k == 0, k == KD - 1)
                ins.then_inc(vproj, 1)

            def turn_ex(p):
                pe.wait_ge(s16_exp, p + 1)
                for m in range(4):
                    ins = pe.transpose(ps[:, TRB, m * P:(m + 1) * P], ex[:, m * P:(m + 1) * P], ident[:])
                ins.then_inc(ex_tr, 1)

            def spread_ex(p, half):
                if half == 0:
                    pe.wait_ge(ex_parts_ok, p + 1)
                if isinstance(p, int) and p == 0:
                    pe.wait_ge(sel_ok, 1)
                for c in range(4 * half, 4 * half + 4):
                    if half == 0 and not (isinstance(p, int) and p == NP - 1):
                        if c == 0:
                            pe.wait_ge(exp_done, p * NCH + 2 * NCH)
                    if c >= 4:
                        pe.wait_ge(prod, p * NC8 + c - 3)
                    pe.matmul(ps[:, c % 4, :], sel[:, c, :], ex_parts[:], start=True, stop=True).then_inc(spread, 1)

            def both(t, cross, pairwise, ending):
                if cross:
                    scores(t, (0, 1))
                if cross:
                    scores(t, (2,))
                if ending:
                    second_part(t - 2)
                if pairwise:
                    norm_t(t - 1)
                if cross:
                    scores(t, (3,))
                if pairwise:
                    pairwise_qk(t - 1)
                    values_y(t - 1)
                if cross:
                    turn_probs(t, pairwise)
                    attend(t, (0, 1))
                if pairwise:
                    pairwise_scores(t - 1)
                if cross:
                    attend(t, (2,))
                if pairwise:
                    turn_ex(t - 1)
                    spread_ex(t - 1, 0)
                if cross:
                    attend(t, (3,))
                if pairwise:
                    spread_ex(t - 1, 1)
                if cross:
                    turn_attended(t)
                if pairwise:
                    first_part(t - 1)
                if cross:
                    project(t)

            both(0, True, False, False)
            both(1, True, True, False)
            with pe.Fori(LOOP, NP) as t:
                both(t, True, True, True)
            both(NP, False, True, True)
            second_part(NP - 1)

            for t in range(NP):
                pe.wait_ge(ln3_ok, t + 1)
                if t >= 2:
                    pe.wait_ge(x3_lo_ok, t - 1)
                elif t == 1:
                    pe.wait_ge(den_ok, 2 * NP)
                for k in range(KD):
                    ins = pe.transpose(ps[:, TRA + t % 2, k * P:(k + 1) * P], n3[t % 2][:, k * P:(k + 1) * P], ident[:])
                ins.then_inc(x3_tr, 1)
            pe.wait_ge(x3_lo_ok, NP)
            pe.wait_ge(gate_split_lo, 1)
            for h in range(2):
                at = slice(h * 512, (h + 1) * 512)
                for k in range(KD):
                    ins = split3(pe, ps[:, OUT + h, :], gate_hi[:, k, :], gate_lo[:, k, :], x3_hi[:, k, at],
                                 x3_lo[:, k, at], k == 0, k == KD - 1)
                ins.then_inc(logit_mm, 1)

            def turn_logits():
                pe.wait_ge(logit_ok, 2)
                for t in range(NP):
                    ins = pe.transpose(ps[:, TRA, t * E:(t + 1) * E], logit_t[:, t * P:(t + 1) * P], ident[0:E, 0:E])
                ins.then_inc(logit_tr, 1)

            def gate_up(s, split, h, slot):
                if h == 0:
                    pe.wait_ge(w_lo_ok, split)
                for n in range(2):
                    if not (isinstance(s, int) and s == 0):
                        pe.wait_ge(h_ok, s * 2 - 1 + n)
                    elif n == 1:
                        turn_logits()
                    for which in range(2):
                        col = which * I + n * P
                        for k in range(KD):
                            wc = k * I2 + col
                            ins = split3(pe, ps[:, 2 * n + which, :], w_hi[slot][:, wc:wc + P],
                                         w_lo[slot][:, wc:wc + P], x3_hi[:, k, h * 512:(h + 1) * 512],
                                         x3_lo[:, k, h * 512:(h + 1) * 512], k == 0, k == KD - 1)
                    ins.then_inc(gu_mm, 1)

            def down(s, split, u, slot):
                pe.wait_ge(w_lo_ok, split)
                pe.wait_ge(h_lo_ok, s * 2 + 2)
                for j in range(4):
                    if not (isinstance(s, int) and s == 0):
                        pe.wait_ge(y_ok, s * 4 - 3 + j)
                    elif j == 0:
                        pe.wait_ge(logits_ok, 1)
                    for n in range(2):
                        wc = KD * I2 + n * D
                        ins = split3(pe, ps[:, 4 + j, :], h_hi[u][:, n, j * P:(j + 1) * P],
                                     h_lo[u][:, n, j * P:(j + 1) * P], w_hi[slot][:, wc:wc + D],
                                     w_lo[slot][:, wc:wc + D], n == 0, n == 1)
                    ins.then_inc(down_mm, 1)

            def four(e2, last):
                for u in range(4):
                    if not (last and u == 3):
                        v = u + 1
                        gate_up(e2 * 4 + v, e2 * 4 + (3 if v < 4 else 5), v % 2, (v // 2) % 2)
                    down(e2 * 4 + u, e2 * 4 + (2 if u < 2 else 4), u % 2, u // 2)

            gate_up(0, 1, 0, 0)
            four(0, False)
            with pe.Fori(1, E // 2 - 1) as e2:
                four(e2, False)
            four(E // 2 - 1, True)


def kernel(**inputs):
    import numpy as np
    import concourse.bacc as bacc
    from concourse.bass_utils import run_bass_kernel_spmd

    def laid(a):
        return np.ascontiguousarray(a)

    i = {k: np.asarray(v) for k, v in inputs.items()}
    arrays = {
        "x": laid(i["x"]),
        "ctx": laid(i["ctx_1024"]),
        "ctx_t": laid(i["ctx_1024"].transpose(0, 2, 1)),
        "wq": laid(i["L0_xattn_Wq"]),
        "bq": laid(i["L0_xattn_bq"].reshape(-1, P).T),
        "wk": laid(i["L0_xattn_Wk"]),
        "bk": laid(i["L0_xattn_bk"].reshape(-1, P).T),
        "wv_t": laid(i["L0_xattn_Wv"].T),
        "bv": laid(i["L0_xattn_bv"]),
        "wqk_t": laid(np.concatenate([i["L0_attn_Wq"], i["L0_attn_Wk"]], 0).T),
        "wphi": laid(i["L0_attn_Wphi"]),
        "wy_t": laid(i["L0_attn_Wy_w"].T),
        "wy_b": laid(i["L0_attn_Wy_b"]),
        "we_t": laid(i["L0_attn_We_w"].T),
        "we_b": laid(i["L0_attn_We_b"]),
        "gate_t": laid(i["L0_ffn_gate_weight"].T),
        "gate_bias": laid(i["L0_ffn_e_score_correction_bias"]),
        "gu_t": laid(np.concatenate([i["L0_ffn_gate_proj"], i["L0_ffn_up_proj"]], 1).transpose(0, 2, 1)),
        "down_t": laid(i["L0_ffn_down_proj"].transpose(0, 2, 1)),
    }
    nc = bacc.Bacc("TRN2", target_bir_lowering=False, num_devices=1)
    named = {f"in_{k}": v for k, v in arrays.items()}
    args = [nc.dram_tensor(k, v.shape, mybir.dt.from_np(v.dtype), kind="ExternalInput").ap() for k, v in named.items()]
    out = nc.dram_tensor("out_0", i["x"].shape, mybir.dt.float32, kind="ExternalOutput").ap()
    perceiver_kernel(nc, *args, out)
    r = run_bass_kernel_spmd(nc, [named], core_ids=[0])
    return r.results[0]["out_0"]
```

```python
from contextlib import ExitStack

import concourse.bass as bass
from concourse import mybir

F32 = mybir.dt.float32
F32R = mybir.dt.float32r
ALU = mybir.AluOpType
ACT = mybir.ActivationFunctionType
AX = mybir.AxisListType
ds = bass.ds

LN_EPS = 1e-5
EPS_RHO = 1e-8
ROOT_EPS_RHO = 1e-4
EPS_DEN = 1e-9
EPS_TOPK = 1e-20

P = 128


def perceiver_kernel(nc, x, ctx, ctx_t, wq, bq, wk, bk, wv_t, bv, wqk_t, wphi, wy_t, wy_b, we_t, we_b,
                     gate_t, gate_bias, gu_t, down_t, out):
    B, SQ, D = x.shape
    SK = ctx.shape[1]
    A = wphi.shape[0]
    E, _, I2 = gu_t.shape
    I = I2 // 2
    KD = D // P
    NP = B * SQ // P
    BP = P // SQ
    NCH = 4
    CW = -(-SK // NCH)
    NT = -(-SK // P)
    TAIL = SK - (NT - 1) * P
    GROUPS = [(0, 4), (4, 7), (7, 10), (10, 13)]
    RING = 10
    NC8 = SQ * SQ // 512
    LOW = 8
    POOL_CONSTS = 14
    assert (B, SQ, D, A, NT, I) == (16, 64, 512, 64, 13, 256) and BP == 2

    def width(c):
        return min(CW, SK - c * CW)

    x_pairs = x.rearrange("(p b) s d -> p (b s) d", b=BP)
    out_rows = out.rearrange("b s d -> (b s) d").rearrange("(t p) d -> t p d", p=P)
    ctx_flat = ctx.rearrange("b t d -> (b t) d")
    ctx_t_rows = ctx_t.rearrange("b (k p) t -> p (b k) t", p=P)

    with ExitStack() as stack:
        base = (nc.sbuf_base + 63) // 64 * 64
        cursor = [base]

        def place(name, shape, dt=F32, at=None):
            n = 4
            for s in shape[1:]:
                n *= s
            where = cursor[0] if at is None else at
            if at is None:
                cursor[0] += (n + 31) // 32 * 32
            return nc.alloc_sbuf_tensor_at(name, shape, dt, offset=where)

        def region(nbytes):
            where = cursor[0]
            cursor[0] += nbytes
            return where

        at_keys = region(NCH * BP * KD * CW * 4)
        keys = place("keys", [P, NCH, BP * KD, CW], at=at_keys)
        WSZ = KD * I2 + (I // P) * D
        w_hi = [place("w_hi0", [P, WSZ], F32R, at=at_keys)]
        w_lo = [place("w_lo0", [P, WSZ], F32R, at=at_keys + WSZ * 4)]
        at_x3a = at_keys + 2 * WSZ * 4
        x3_hi = [place("x3a_hi", [P, KD, 512], F32R, at=at_x3a)]
        x3_lo = [place("x3a_lo", [P, KD, 512], F32R, at=at_x3a + 8192)]
        gu_raw = [place("gu_raw0", [P, KD, I2], at=at_x3a + 16384)]
        gate_hi = place("gate_hi", [P, KD, P], F32R, at=at_x3a + 24576)
        x1t_lo2 = place("x1t_lo2", [P, KD, 512], F32R, at=at_keys + (NCH - 1) * BP * KD * CW * 4)
        at_vals = region(BP * RING * D * 4)
        vals = place("vals", [P, RING, BP, D], at=at_vals)
        wq_sb = place("wq_sb", [P, KD, D], at=at_vals)
        wk_sb = place("wk_sb", [P, KD, D], at=at_vals + 8192)
        bq_rep = place("bq_rep", [P, KD, P], at=at_vals + 36864)
        bk_rep = place("bk_rep", [P, KD, P], at=at_vals + 32768)
        v_rep = place("v_rep", [P, D], at=at_vals + 34816)
        w_hi.append(place("w_hi1", [P, WSZ], F32R, at=at_vals))
        w_lo.append(place("w_lo1", [P, WSZ], F32R, at=at_vals + WSZ * 4))
        x3_hi.append(place("x3b_hi", [P, KD, 512], F32R, at=at_vals + 2 * WSZ * 4))
        x3_lo.append(place("x3b_lo", [P, KD, 512], F32R, at=at_vals + 2 * WSZ * 4 + 8192))
        at_proj = region(4 * KD * D * 4)
        wv_hi = place("wv_hi", [P, KD, D], F32R, at=at_proj)
        wv_lo = place("wv_lo", [P, KD, D], F32R, at=at_proj + 8192)
        wv_raw = place("wv_raw", [P, KD, D], F32, at=at_proj + 8192)
        wy_hi = place("wy_hi", [P, KD, D], F32R, at=at_proj + 16384)
        wy_lo = place("wy_lo", [P, KD, D], F32R, at=at_proj + 24576)
        wy_raw = place("wy_raw", [P, KD, D], F32, at=at_proj + 24576)
        dn_raw = [place(f"dn_raw{s}", [P, I // P, D], at=at_proj + 4096 * s) for s in range(2)]
        h_hi = [place(f"h_hi{s}", [P, 2, 512], F32R, at=at_proj + 8192 + s * 8192) for s in range(2)]
        h_lo = [place(f"h_lo{s}", [P, 2, 512], F32R, at=at_proj + 12288 + s * 8192) for s in range(2)]
        silu_sb = place("silu_sb", [P, 2, 512], at=at_proj + 24576)
        h_sb = place("h_sb", [P, 2, 512], at=at_proj + 28672)
        at_plane = region(SQ * SQ * 4)
        plane = place("plane", [P, SQ * SQ], at=at_plane)
        x1t_hi = place("x1t_hi", [P, KD, 512], F32R, at=at_plane)
        x1t_lo = place("x1t_lo", [P, KD, 512], F32R, at=at_plane + 8192)
        logit_t = place("logit_t", [E, NP * P], at=at_plane + 8192)
        beat = place("beat", [P, NP, E, E], at=at_plane + 12288)
        tie = place("tie", [P, NP, E, E], at=at_plane + 14336)
        rows = place("rows", [P, NP * D])
        rows3 = rows[:, :].rearrange("p (n d) -> p n d", d=D)
        at_probs = cursor[0]
        m_hi = place("m_hi", [P, KD, D], F32R, at=at_probs)
        m_lo = place("m_lo", [P, KD, D], F32R, at=at_probs + 8192)
        x1t_hi2 = place("x1t_hi2", [P, KD, 512], F32R, at=at_probs + 16384)
        probs = place("probs", [P, SK])
        gate_sb = place("gate_sb", [P, KD, P], at=at_probs)
        n3 = [place(f"n3_{s}", [P, D], at=at_probs + 2048 * (s + 1)) for s in range(2)]
        probs_t = place("probs_t", [P, NT, P])
        at_late = [cursor[0] - NT * P * 4]
        x_in = place("x_in", [P, D])
        gu_raw.append(place("gu_raw1", [P, KD, I2], at=cursor[0] - 2048))
        norm = place("norm", [P, D])
        nt_hi = place("nt_hi", [P, KD, P], F32R)
        nt_lo = place("nt_lo", [P, KD, P], F32R)
        nt_f = place("nt_f", [P, KD, P])
        vy = place("vy", [P, D])
        assert cursor[0] >= at_probs + 24576
        gate_lo = place("gate_lo", [P, KD, P], F32R, at=cursor[0])
        q_cur = place("q_cur", [P, KD, P])
        bv_b = place("bv_b", [P, D])
        bwe_b = place("bwe_b", [P, D])
        we2 = place("we2", [P, D])
        wqk_sb = place("wqk_sb", [P, KD, P])
        sel = place("sel", [P, NC8, P], F32R)
        ex = place("ex", [P, 512])
        at_exs = region(4096)
        ex_hi = place("ex_hi", [P, 512], F32R, at=at_exs)
        ex_parts = place("ex_parts", [P, 512], F32R, at=at_exs + 2048)
        sel_f = place("sel_f", [P, NC8, P], at=at_exs)
        ex_t = place("ex_t", [P, P])
        ew_t = place("ew_t", [P, P])
        ew = place("ew", [P, SQ])
        ident = place("ident", [P, P])
        phi_sel = place("phi_sel", [P, 2, 32])
        tmp = place("tmp", [P, D])
        q2 = place("q2", [P, SQ])
        k2 = place("k2", [P, SQ])
        small = {}
        for name, n in (("ones", 2), ("bq_c", KD), ("bk_c", KD), ("kbias", KD), ("cq", NP), ("c0", 1), ("phi_c", 1),
                        ("low_rows", 16), ("minus_low", 1), ("eps_ln", 1), ("eps_rho", 1),
                        ("mx", NCH), ("mx1", 1), ("smax", 1), ("ebias", 1), ("sums", NCH), ("ssum", 1), ("rinv", 1),
                        ("st3", 6 * NP), ("mv3", 2 * NP), ("sd3", NP), ("rs3", NP),
                        ("st1", 6 * NP), ("mv1", 2 * NP), ("sd1", NP),
                        ("rs1", NP), ("st2", 6), ("mv2", 2), ("sd2", 1), ("rs2", 1), ("mx16", 8), ("den", 1),
                        ("den1", 1), ("rden", 1)):
            small[name] = place(name, [P, n])
        small["gbias"] = place("gbias", [P, E])
        small["before"] = place("before", [P, E * E])
        for name, n in (("logits", NP * E), ("score", NP * E), ("choice", NP * E),
                        ("grp", NP * E // 2), ("grank", NP * E // 2), ("gmask", NP * E // 2), ("kept", NP * E),
                        ("rank", NP * E), ("wsel", NP * E), ("wsum", NP), ("winv", NP), ("comb", E * NP),
                        ("comb_e0", NP), ("comb_e1", NP)):
            small[name] = place(name, [P, n], at=at_late[0])
            at_late[0] += (n * 4 + 31) // 32 * 32
        assert cursor[0] <= nc.sbuf_usable_end, cursor[0]

        ps = stack.enter_context(nc.psum_tensor("ps", [P, 8, 512], F32))
        TRA, TRB, OUT, ACC = 4, 5, 6, 7

        def sem(name):
            return stack.enter_context(nc.semaphore(name))

        x_all_in, bias_in = sem("x_all_in"), sem("bias_in")
        wqk_in = [sem(f"wqk_in{k}") for k in range(KD)]
        x_all_in2 = sem("x_all_in2")
        wv_in, wy_in, small_in = sem("wv_in"), sem("wy_in"), sem("small_in")
        keys_in = [sem(f"keys_in{c}") for c in range(NCH)]
        vals_in = [sem(f"vals_in{g}") for g in range(len(GROUPS))]
        x_in_sem = sem("x_in_sem")
        gu_in = [sem(f"gu_in{s}") for s in range(2)]
        dn_in = [sem(f"dn_in{s}") for s in range(2)]
        gate_in, gate_zero = sem("gate_in"), sem("gate_zero")
        out_done = sem("out_done")
        pool_const, bk_rep_ok, phi_ok, bwe_ok, vec_const = (sem("pool_const"), sem("bk_rep_ok"), sem("phi_ok"),
                                                            sem("bwe_ok"), sem("vec_const"))
        sel_ok, low_rows_ok = sem("sel_ok"), sem("low_rows_ok")
        m_mm, m_hi_ok, m_lo_ok, vrep_mm, bias_mm, bias_ok = (sem("m_mm"), sem("m_hi_ok"), sem("m_lo_ok"),
                                                             sem("vrep_mm"), sem("bias_mm"), sem("bias_ok"))
        ln1_stat, ln1_sd, ln1_rs, ln1_ok, ln1_tr, ln1_hi, ln1_lo, cq_ok = (
            sem("ln1_stat"), sem("ln1_sd"), sem("ln1_rs"), sem("ln1_ok"), sem("ln1_tr"), sem("ln1_hi"),
            sem("ln1_lo"), sem("cq_ok"))
        q_mm, q_ok = sem("q_mm"), sem("q_ok")
        wsplit_hi, wsplit_lo = sem("wsplit_hi"), sem("wsplit_lo")
        q_ready, xb_ready, scored, max_step, ebias_ok, exp_done = (sem("q_ready"), sem("xb_ready"), sem("scored"),
                                                                   sem("max_step"), sem("ebias_ok"), sem("exp_done"))
        probs_tr, pt_act, pt_dve, pv_done, rinv_step, attended_ok = (sem("probs_tr"), sem("pt_act"), sem("pt_dve"),
                                                                     sem("pv_done"), sem("rinv_step"),
                                                                     sem("attended_ok"))
        o_tr, o_hi, o_lo, vproj, x1_ok, ln2_stat, ln2_sd, ln2_rs, ln2_ok = (
            sem("o_tr"), sem("o_hi"), sem("o_lo"), sem("vproj"), sem("x1_ok"), sem("ln2_stat"), sem("ln2_sd"),
            sem("ln2_rs"), sem("ln2_ok"))
        n_tr, n_f, n_hi, n_lo, qk_mm, qk_ok, vy_mm, vy_ok = (sem("n_tr"), sem("n_f"), sem("n_hi"), sem("n_lo"),
                                                             sem("qk_mm"), sem("qk_ok"), sem("vy_mm"), sem("vy_ok"))
        z_ok, relu_ok, root_ok, s16_mm, s16_max, s16_sub, s16_exp, ex_hi_ok, ex_parts_ok = (
            sem("z_ok"), sem("relu_ok"), sem("root_ok"), sem("s16_mm"), sem("s16_max"),
            sem("s16_sub"), sem("s16_exp"), sem("ex_hi_ok"), sem("ex_parts_ok"))
        ex_tr, ex_t_ok, spread, prod, ew_red, ew_ok, den_mm, den_ok, rden_ok, part_mm, tmp_ok, x2_ok = (
            sem("ex_tr"), sem("ex_t_ok"), sem("spread"), sem("prod"), sem("ew_red"), sem("ew_ok"), sem("den_mm"),
            sem("den_ok"), sem("rden_ok"), sem("part_mm"), sem("tmp_ok"), sem("x2_ok"))
        st3_ok = sem("st3_ok")
        ln3_stat, ln3_sd, ln3_rs, ln3_ok, x3_tr, x3_hi_ok, x3_lo_ok = (
            sem("ln3_stat"), sem("ln3_sd"), sem("ln3_rs"), sem("ln3_ok"), sem("x3_tr"), sem("x3_hi_ok"),
            sem("x3_lo_ok"))
        gate_split_hi, gate_split_lo, logit_mm, logit_ok, logit_tr, logits_ok, score_ok, gate_step = (
            sem("gate_split_hi"), sem("gate_split_lo"), sem("logit_mm"), sem("logit_ok"), sem("logit_tr"),
            sem("logits_ok"), sem("score_ok"), sem("gate_step"))
        w_hi_ok, w_lo_ok, gu_mm, silu_ok, h_ok, h_hi_ok, h_lo_ok, down_mm, y_ok, comb_ok = (
            sem("w_hi_ok"), sem("w_lo_ok"), sem("gu_mm"), sem("silu_ok"), sem("h_ok"), sem("h_hi_ok"),
            sem("h_lo_ok"), sem("down_mm"), sem("y_ok"), sem("comb_ok"))

        block = stack.enter_context(nc.Block())
        LOOP = 2
        EARLY3 = 6
        X3_BANK = [TRA, ACC, TRA, 2, TRA, TRA, TRA, TRB]

        def last_pair(t):
            return isinstance(t, int) and t == NP - 1

        def x3_part(parts, t):
            return parts[t // 4][:, :, (t % 4) * P:(t % 4 + 1) * P]

        def x3_bank(t):
            return ps[:, X3_BANK[t], :].rearrange("p (k n) -> p k n", k=KD)

        def row(p):
            return rows[:, ds(p * D, D)]

        def wait_apart(eng, semaphore, value):
            if not isinstance(value, int):
                value = eng.snap(value)
            eng.wait_ge(x_all_in, 16)
            eng.wait_ge(semaphore, value)

        def split3(pe, out_ap, left_hi, left_lo, right_hi, right_lo, first, last):
            pe.matmul(out_ap, left_hi, right_hi, start=first, stop=False)
            pe.matmul(out_ap, left_hi, right_lo, start=False, stop=False)
            return pe.matmul(out_ap, left_lo, right_hi, start=False, stop=last)

        SPLITS = [("gu", 0), ("gu", 1), ("down", 0), ("down", 1)]

        def expert_part(which, s):
            if which == "gu":
                return gu_raw[s][:, :, :].rearrange("p k n -> p (k n)"), slice(0, KD * I2)
            return dn_raw[s][:, :, :].rearrange("p k n -> p (k n)"), slice(KD * I2, WSZ)

        @block.sync
        def _(sp):
            half = NP // 2
            x_rows = x_pairs.rearrange("n p d -> p n d")
            for k in range(KD):
                sp.dma_start(wq_sb[:, k, :], wq[k * P:(k + 1) * P, :]).then_inc(wqk_in[k], 16)
            sp.dma_start(rows3[:, 0:half, :], x_rows[:, 0:half, :]).then_inc(x_all_in, 16)
            sp.dma_start(rows3[:, half:, :], x_rows[:, half:, :]).then_inc(x_all_in2, 16)

            def load_keys(p, c):
                if not (isinstance(p, int) and p == 0):
                    sp.wait_ge(scored, p * NCH - NCH + c + 1)
                sp.dma_start(keys[:, c, :, 0:width(c)],
                             ctx_t_rows[:, ds(p * (BP * KD), BP * KD), c * CW:c * CW + width(c)]
                             ).then_inc(keys_in[c], 16)

            def load_vals(p, g):
                lo, hi = GROUPS[g]
                slot = lo % RING
                if g == 3:
                    sp.wait_ge(pv_done, p * 4 + 1)
                elif not (isinstance(p, int) and p == 0):
                    sp.wait_ge(pv_done, p * 4)
                for b in range(BP):
                    full = hi - lo if hi < NT else hi - lo - 1
                    start = (p * BP + b) * SK
                    sp.dma_start(vals[:, slot:slot + full, b, :],
                                 ctx_flat[ds(start + lo * P, full * P), :].rearrange("(n p) d -> p n d", p=P)
                                 ).then_inc(vals_in[g], 16)
                    if hi == NT:
                        sp.dma_start(vals[0:TAIL, slot + full, b, :],
                                     ctx_flat[ds(start + (NT - 1) * P, TAIL), :]).then_inc(vals_in[g], 16)

            def load_x(p):
                if not (isinstance(p, int) and p == 0):
                    sp.wait_ge(x1_ok, p)
                sp.dma_start(x_in[:], x_pairs[p]).then_inc(x_in_sem, 16)

            load_keys(0, 0)
            load_keys(0, 1)
            sp.dma_start(wv_raw[:], wv_t.rearrange("(k p) n -> p k n", p=P)).then_inc(wv_in, 16)
            sp.dma_start(wy_raw[:], wy_t.rearrange("(k p) n -> p k n", p=P)).then_inc(wy_in, 16)
            load_keys(0, 2)
            sp.wait_ge(vrep_mm, 1)
            sp.wait_ge(bias_mm, 2)
            load_vals(0, 0)
            load_vals(0, 1)
            sp.wait_ge(cq_ok, NP)
            load_vals(0, 2)
            sp.wait_ge(q_mm, 2 * KD)
            load_keys(0, 3)
            load_x(0)
            load_vals(0, 3)

            def pair_loads(p):
                load_keys(p, 0)
                load_keys(p, 1)
                load_keys(p, 2)
                load_keys(p, 3)
                load_x(p)
                for g in range(4):
                    load_vals(p, g)

            with sp.Fori(1, NP) as p:
                pair_loads(p)

            def load_gu(e, s):
                sp.dma_start(gu_raw[s][:], gu_t[e].rearrange("(k p) n -> p k n", p=P)).then_inc(gu_in[s], 16)

            def load_down(e, s):
                sp.dma_start(dn_raw[s][:], down_t[e].rearrange("(k p) n -> p k n", p=P)).then_inc(dn_in[s], 16)

            sp.wait_ge(scored, NP * NCH)
            load_gu(0, 0)
            sp.wait_ge(vproj, NP)
            load_down(0, 0)
            load_down(1, 1)
            sp.wait_ge(vy_mm, NP)
            load_gu(1, 1)
            with sp.Fori(1, E // 2) as e2:
                for n, (which, s) in enumerate(SPLITS):
                    sp.wait_ge(w_lo_ok, e2 * 4 - 3 + n)
                    (load_gu if which == "gu" else load_down)(e2 * 2 + s, s)
            for t in range(NP):
                step = 2 * E - 3 + 2 * (t // 4)
                sp.wait_ge(y_ok, step * 4 + t % 4 + 1)
                sp.dma_start(out_rows[t], rows3[:, t, :]).then_inc(out_done, 16)
            sp.wait_ge(out_done, NP * 16)

        @block.gpsimd
        def _(pool):
            pool.memset(ident[:], 0.0).then_inc(pool_const, 1)
            pool.memset(sel_f[:], 0.0).then_inc(pool_const, 1)
            pool.memset(ex_t[:], 0.0).then_inc(pool_const, 1)
            pool.memset(ew_t[:], 0.0).then_inc(pool_const, 1)
            pool.memset(phi_sel[:], 0.0).then_inc(pool_const, 1)
            pool.memset(small["before"][:], 1.0).then_inc(pool_const, 1)
            pool.memset(small["low_rows"][:], 0.0).then_inc(pool_const, 1)
            pool.wait_ge(pool_const, 7)
            pool.affine_select(out=ident[:], in_=ident[:], compare_op=ALU.not_equal, fill=1.0, base=0,
                               pattern=[[-1, P]], channel_multiplier=1).then_inc(pool_const, 1)
            bf = small["before"][:, :].rearrange("p (e f) -> p e f", e=E)
            pool.affine_select(out=bf, in_=bf, compare_op=ALU.is_gt, fill=0.0, base=0,
                               pattern=[[1, E], [-1, E]], channel_multiplier=0).then_inc(pool_const, 1)
            for low in range(2):
                if low:
                    pool.wait_ge(pool_const, 11)
                for b in range(BP):
                    v = sel_f[:, :, b * A:(b + 1) * A].rearrange("p (g j) a -> p g j a", j=4)
                    pool.affine_select(out=v, in_=v, compare_op=ALU.not_equal, fill=1.0, base=-b - LOW * low,
                                       pattern=[[-2, 2], [-32, 4], [0, A]], channel_multiplier=1
                                       ).then_inc(pool_const, 1)
            v = small["low_rows"][:, :].rearrange("p (j r) -> p j r", j=4)
            pool.affine_select(out=v, in_=v, compare_op=ALU.not_equal, fill=-1.0, base=-LOW,
                               pattern=[[-32, 4], [-1, 4]], channel_multiplier=1).then_inc(pool_const, 1)

            def pair_inputs(p):
                if not (isinstance(p, int) and p == 0):
                    wait_apart(pool, scored, p * NCH)
                pool.tensor_copy(q_cur[:, :, :].rearrange("p k n -> p (k n)"), row(p)).then_inc(q_ready, 1)
                pool.wait_ge(x_in_sem, p * 16 + 16)
                pool.tensor_tensor(x_in[:], x_in[:], bv_b[:], ALU.add).then_inc(xb_ready, 1)

            def fill_plane(p):
                pool.wait_ge(qk_ok, p + 1)
                h = SQ // 2
                for half in range(2):
                    z = plane[:, half * h * SQ:(half + 1) * h * SQ].rearrange("p (i j) -> p i j", j=SQ)
                    pool.tensor_tensor(z, q2[:, half * h:(half + 1) * h].unsqueeze(2).to_broadcast([P, h, SQ]),
                                       k2[:, :].unsqueeze(1).to_broadcast([P, h, SQ]), ALU.add).then_inc(z_ok, 1)

            pool.wait_ge(x_all_in, 16)
            pool.wait_ge(q_ok, KD)
            pool.wait_ge(small_in, 16 * 9)
            pair_inputs(0)
            pool.wait_ge(q_ok, 2 * KD)
            with pool.Fori(1, NP) as p:
                pair_inputs(p)
                fill_plane(p - 1)

            def low_part(which, s, count):
                raw, at = expert_part(which, s)
                pool.wait_ge(w_hi_ok, count)
                pool.tensor_tensor(w_lo[s][:, at], raw, w_hi[s][:, at].bitcast(F32), ALU.subtract).then_inc(w_lo_ok, 1)

            pool.wait_ge(probs_tr, NP * 4)
            pool.memset(gate_sb[:], 0.0).then_inc(gate_zero, 1)
            low_part("gu", 0, 1)
            fill_plane(NP - 1)
            for n in range(1, 4):
                low_part(*SPLITS[n], n + 1)
            with pool.Fori(1, E // 2) as e2:
                for n, (which, s) in enumerate(SPLITS):
                    low_part(which, s, e2 * 4 + 1 + n)

        @block.scalar
        def _(act):
            for k in range(KD):
                act.dma_start(wk_sb[:, k, :], wk[k * P:(k + 1) * P, :]).then_inc(wqk_in[k], 16)
                if k == 0:
                    act.dma_start(small["bq_c"][:], bq).then_inc(bias_in, 16)
                    act.dma_start(small["bk_c"][:], bk).then_inc(bias_in, 16)
            act.dma_start(bv_b[:], bv.partition_broadcast(P)).then_inc(small_in, 16)
            act.dma_start(bwe_b[:], we_b.partition_broadcast(P)).then_inc(small_in, 16)
            act.dma_start(tmp[:], wy_b.partition_broadcast(P)).then_inc(small_in, 16)
            act.dma_start(small["gbias"][:], gate_bias.partition_broadcast(P)).then_inc(small_in, 16)
            act.dma_start(wqk_sb[:], wqk_t.rearrange("(k p) n -> p k n", p=P)).then_inc(small_in, 16)
            for b in range(BP):
                act.dma_start(we2[b * A:(b + 1) * A, :], we_t).then_inc(small_in, 16)
                act.dma_start(small["phi_c"][b * A:(b + 1) * A, :], wphi.rearrange("(a n) -> a n", n=1)
                              ).then_inc(small_in, 16)

            def root_of_var(out_ap, var_ap, done):
                act.activation(out_ap, var_ap, ACT.Sqrt, bias=small["eps_ln"][:, 0:1]).then_inc(done, 1)

            act.wait_ge(ln1_stat, NP)
            root_of_var(small["sd1"][:], small["mv1"][:, :].rearrange("p (n t) -> p n t", t=2)[:, :, 1], ln1_sd)
            for m in range(KD):
                act.wait_ge(m_mm, m + 1)
                act.copy(m_hi[:, m, :], ps[:, m, :]).then_inc(m_hi_ok, 1)
            for t in range(NP):
                act.wait_ge(ln1_tr, t + 1)
                act.copy((x1t_hi if t < 4 else x1t_hi2)[:, :, (t % 4) * P:(t % 4 + 1) * P],
                         ps[:, OUT + t % 2, :].rearrange("p (k n) -> p k n", k=KD)).then_inc(ln1_hi, 1)
            act.wait_ge(wv_in, 16)
            act.copy(wv_hi[:], wv_raw[:]).then_inc(wsplit_hi, 1)
            act.wait_ge(wy_in, 16)
            act.copy(wy_hi[:], wy_raw[:]).then_inc(wsplit_hi, 1)
            act.wait_ge(pool_const, POOL_CONSTS)
            act.copy(sel[:], sel_f[:]).then_inc(sel_ok, 1)

            def exp_scores(p):
                if not (isinstance(p, int) and p == 0):
                    act.wait_ge(probs_tr, p * 4)
                    act.wait_ge(rinv_step, p * 2)
                act.wait_ge(ebias_ok, p + 1)
                for c in range(NCH):
                    act.activation(probs[:, c * CW:c * CW + width(c)], ps[:, c, 0:width(c)], ACT.Exp,
                                   bias=small["ebias"][:, 0:1], accum_out=small["sums"][:, c:c + 1]
                                   ).then_inc(exp_done, 1)

            def copy_norm_t(p):
                act.wait_ge(n_tr, p + 1)
                v = ps[:, TRA, :].rearrange("p (k n) -> p k n", k=KD)
                act.copy(nt_f[:], v).then_inc(n_f, 1)
                act.copy(nt_hi[:], v).then_inc(n_hi, 1)

            def copy_vy(p):
                act.wait_ge(vy_mm, p + 1)
                act.copy(vy[:], ps[:, ACC, :]).then_inc(vy_ok, 1)

            def copy_probs_t(p):
                for g in (1, 3):
                    lo, hi = GROUPS[g]
                    full = hi - lo if hi < NT else hi - lo - 1
                    act.wait_ge(probs_tr, p * 4 + g + 1)
                    ins = act.copy(probs_t[:, lo:lo + full, :],
                                   ps[:, TRB, 0:full * P].rearrange("p (k n) -> p k n", n=P))
                    if hi == NT:
                        ins = act.copy(probs_t[0:TAIL, NT - 1, :], ps[0:TAIL, TRB, full * P:(full + 1) * P])
                    ins.then_inc(pt_act, 1)

            def roots(p):
                for h in range(2):
                    act.wait_ge(relu_ok, p * 2 + h + 1)
                    v = plane[:, h * 2048:(h + 1) * 2048]
                    act.activation(v, v, ACT.Sqrt, bias=small["eps_rho"][:, 0:1]).then_inc(root_ok, 1)

            def copy_o_t(p):
                act.wait_ge(o_tr, p + 1)
                act.copy(nt_hi[:], ps[:, TRA, :].rearrange("p (k n) -> p k n", k=KD)).then_inc(o_hi, 1)

            def exp_pairwise(p):
                act.wait_ge(s16_sub, p + 1)
                act.activation(ex[:], ex[:], ACT.Exp).then_inc(s16_exp, 1)
                act.wait_ge(s16_exp, p + 1)
                act.copy(ex_hi[:], ex[:]).then_inc(ex_hi_ok, 1)

            def root2(p):
                act.wait_ge(ln2_stat, p * 2 + 2)
                root_of_var(small["sd2"][:], small["mv2"][:, 1:2], ln2_sd)

            def root3(lo, hi):
                act.wait_ge(ln3_stat, hi)
                root_of_var(small["sd3"][:, lo:hi],
                            small["mv3"][:, :].rearrange("p (n t) -> p n t", t=2)[:, lo:hi, 1], ln3_sd)

            def high_x3(t):
                act.wait_ge(x3_tr, t + 1)
                act.copy(x3_part(x3_hi, t), x3_bank(t)).then_inc(x3_hi_ok, 1)

            def high_part(which, s, fills):
                raw, at = expert_part(which, s)
                act.wait_ge((gu_in if which == "gu" else dn_in)[s], fills * 16)
                act.copy(w_hi[s][:, at], raw).then_inc(w_hi_ok, 1)

            def silu(s, n):
                act.wait_ge(gu_mm, s * 2 + n + 1)
                if not (isinstance(s, int) and s == 0):
                    act.wait_ge(h_ok, s * 2 - 1 + n)
                act.activation(silu_sb[:, n, :], ps[:, 2 * n, :], ACT.Silu).then_inc(silu_ok, 1)

            def high_h(s, u):
                for n in range(2):
                    act.wait_ge(h_ok, s * 2 + n + 1)
                    if not (isinstance(s, int) and s < 2):
                        act.wait_ge(down_mm, s * 4 - 4)
                    act.copy(h_hi[u][:, n, :], h_sb[:, n, :]).then_inc(h_hi_ok, 1)

            def both(t, cross, pairwise):
                if pairwise:
                    copy_norm_t(t - 1)
                if cross:
                    exp_scores(t)
                if cross:
                    copy_probs_t(t)
                if last_pair(t):
                    root3(0, EARLY3)
                if pairwise:
                    roots(t - 1)
                    copy_vy(t - 1)
                if last_pair(t):
                    high_x3(0)
                if pairwise:
                    exp_pairwise(t - 1)
                if last_pair(t):
                    high_x3(1)
                    high_part("gu", 0, 1)
                    high_x3(2)
                if cross:
                    copy_o_t(t)
                if last_pair(t):
                    high_x3(3)
                if cross:
                    root2(t)

            both(0, True, False)
            both(1, True, True)
            with act.Fori(LOOP, NP - 1) as t:
                both(t, True, True)
            both(NP - 1, True, True)

            act.wait_ge(gate_zero, 1)
            act.dma_start(gate_sb[:, :, 0:E], gate_t.rearrange("(k p) n -> p k n", p=P)).then_inc(gate_in, 16)
            copy_norm_t(NP - 1)
            roots(NP - 1)
            copy_vy(NP - 1)
            high_x3(4)
            act.wait_ge(gate_in, 16)
            act.copy(gate_hi[:], gate_sb[:]).then_inc(gate_split_hi, 1)
            silu(0, 0)
            silu(0, 1)
            high_h(0, 0)
            exp_pairwise(NP - 1)
            high_x3(5)
            high_part("gu", 1, 1)
            high_part("down", 0, 1)
            silu(1, 0)
            root3(EARLY3, NP)
            silu(1, 1)
            high_x3(6)
            high_x3(7)
            high_h(1, 1)
            for h in range(2):
                act.wait_ge(logit_mm, h + 1)
                if h == 0:
                    act.wait_ge(ew_red, 2 * NP)
                act.copy(logit_t[:, h * 512:(h + 1) * 512], ps[0:E, ACC - h, :]).then_inc(logit_ok, 1)
            act.wait_ge(logits_ok, 1)
            act.activation(small["score"][:], small["logits"][:], ACT.Sigmoid).then_inc(score_ok, 1)
            high_part("down", 1, 1)

            def silu_step(s, u):
                silu(s, 0)
                silu(s, 1)
                high_h(s, u)

            def second_half(e2, last):
                silu_step(e2 * 4 + 2, 0)
                if not last:
                    high_part("gu", 0, e2 + 2)
                silu_step(e2 * 4 + 3, 1)
                if not last:
                    high_part("gu", 1, e2 + 2)
                    act.wait_ge(down_mm, e2 * 16 + 12)
                    high_part("down", 0, e2 + 2)

            def first_half(e2):
                silu_step(e2 * 4, 0)
                act.wait_ge(down_mm, e2 * 16)
                high_part("down", 1, e2 + 1)
                silu_step(e2 * 4 + 1, 1)

            second_half(0, False)
            with act.Fori(1, E // 2 - 1) as e2:
                first_half(e2)
                second_half(e2, False)
            first_half(E // 2 - 1)
            second_half(E // 2 - 1, True)

        @block.vector
        def _(dve):
            sm = small
            dve.memset(sm["ones"][:], 1.0).then_inc(vec_const, 1)
            dve.memset(sm["eps_ln"][:], LN_EPS).then_inc(vec_const, 1)
            dve.memset(sm["eps_rho"][:], EPS_RHO).then_inc(vec_const, 1)
            dve.memset(bk_rep[:], 1.0).then_inc(vec_const, 1)
            dve.memset(bq_rep[:], 1.0).then_inc(vec_const, 1)
            dve.wait_ge(vec_const, 5)
            dve.wait_ge(bias_in, 32)
            for k in range(KD):
                dve.tensor_scalar(bq_rep[:, k, :], bq_rep[:, k, :], sm["bq_c"][:, k:k + 1], None, ALU.mult)
                ins = dve.tensor_scalar(bk_rep[:, k, :], bk_rep[:, k, :], sm["bk_c"][:, k:k + 1], None, ALU.mult)
            ins.then_inc(bk_rep_ok, 1)
            for t in range(NP):
                if t == 0:
                    dve.wait_ge(x_all_in, 16)
                elif t == NP // 2:
                    dve.wait_ge(x_all_in2, 16)
                dve.bn_stats(sm["st1"][:, 6 * t:6 * t + 6], rows3[:, t, :]).then_inc(ln1_rs, 1)
            for t in range(NP):
                dve.wait_ge(ln1_rs, t + 1)
                dve.bn_aggr(sm["mv1"][:, 2 * t:2 * t + 2], sm["st1"][:, 6 * t:6 * t + 6]).then_inc(ln1_stat, 1)
            dve.wait_ge(ln1_sd, 1)
            dve.reciprocal(sm["rs1"][:], sm["sd1"][:]).then_inc(ln1_rs, 1)
            dve.wait_ge(ln1_rs, NP + 1)
            for t in range(NP):
                dve.tensor_scalar(rows3[:, t, :], rows3[:, t, :], sm["mv1"][:, 2 * t:2 * t + 1],
                                  sm["rs1"][:, t:t + 1], ALU.subtract, ALU.mult).then_inc(ln1_ok, 1)
            for m in range(KD):
                dve.wait_ge(m_hi_ok, m + 1)
                dve.tensor_tensor(m_lo[:, m, :], ps[:, m, :], m_hi[:, m, :].bitcast(F32), ALU.subtract
                                  ).then_inc(m_lo_ok, 1)
            for t in range(NP):
                if t == 1:
                    dve.wait_ge(vrep_mm, 1)
                    dve.tensor_copy(v_rep[:], ps[:, TRA, :]).then_inc(bias_ok, 1)
                elif t == 4:
                    dve.wait_ge(bias_mm, 1)
                    dve.tensor_copy(sm["kbias"][:], ps[:, TRB, :].rearrange("p (m n) -> p m n", n=P)[:, :, 0]
                                    ).then_inc(bias_ok, 1)
                elif t == 5:
                    dve.wait_ge(bias_mm, 2)
                    dve.tensor_copy(sm["c0"][:], ps[:, TRA, 0:1]).then_inc(bias_ok, 1)
                at = slice((t % 4) * P, (t % 4 + 1) * P)
                hi, lo = (x1t_hi, x1t_lo) if t < 4 else (x1t_hi2, x1t_lo2)
                dve.wait_ge(ln1_hi, t + 1)
                dve.tensor_tensor(lo[:, :, at], ps[:, OUT + t % 2, :].rearrange("p (k n) -> p k n", k=KD),
                                  hi[:, :, at].bitcast(F32), ALU.subtract).then_inc(ln1_lo, 1)
            dve.wait_ge(ln1_ok, NP)
            dve.wait_ge(bias_ok, 3)
            for t in range(NP):
                dve.tensor_tensor_reduce(out=ex[:], in0=rows3[:, t, :],
                                         in1=v_rep[:], scale=1.0, scalar=0.0, op0=ALU.mult, op1=ALU.add,
                                         accum_out=sm["cq"][:, t:t + 1]).then_inc(cq_ok, 1)
                dve.wait_ge(cq_ok, t + 1)
            dve.tensor_scalar(sm["cq"][:], sm["cq"][:], sm["c0"][:, 0:1], None, ALU.add).then_inc(cq_ok, 1)
            for h in range(2):
                for m in range(KD):
                    dve.wait_ge(q_mm, h * KD + m + 1)
                    dve.tensor_scalar(rows3[:, 4 * h:4 * h + 4, m * P:(m + 1) * P],
                                      ps[:, 4 * h + m, :].rearrange("p (t n) -> p t n", t=4),
                                      sm["kbias"][:, m:m + 1], None, ALU.add).then_inc(q_ok, 1)
            dve.wait_ge(wsplit_hi, 1)
            dve.tensor_tensor(wv_lo[:], wv_raw[:], wv_hi[:].bitcast(F32), ALU.subtract).then_inc(wsplit_lo, 1)
            dve.wait_ge(wsplit_hi, 2)
            dve.tensor_tensor(wy_lo[:], wy_raw[:], wy_hi[:].bitcast(F32), ALU.subtract).then_inc(wsplit_lo, 1)
            dve.wait_ge(small_in, 16 * 9)
            dve.wait_ge(pool_const, POOL_CONSTS)
            dve.reduce_sum(sm["minus_low"][:], sm["low_rows"][:], AX.X).then_inc(low_rows_ok, 1)
            for b in range(BP):
                for g in range(2):
                    for at in (g * 2 + b, LOW + g * 2 + b):
                        dve.tensor_copy(phi_sel[b * A:(b + 1) * A, g, at:at + 1], sm["phi_c"][b * A:(b + 1) * A, :]
                                        ).then_inc(phi_ok, 1)
            dve.tensor_tensor(bwe_b[:], bwe_b[:], tmp[:], ALU.add).then_inc(bwe_ok, 1)
            dve.wait_ge(cq_ok, NP + 1)
            dve.wait_ge(low_rows_ok, 1)
            dve.wait_ge(bwe_ok, 1)

            def chunk_max(p, c):
                dve.wait_ge(scored, p * NCH + c + 1)
                dve.reduce_max(sm["mx"][:, c:c + 1], ps[:, c, 0:width(c)], AX.X).then_inc(max_step, 1)

            def row_max(p):
                dve.wait_ge(max_step, p * 6 + 4)
                dve.reduce_max(sm["mx1"][:], sm["mx"][:], AX.X).then_inc(max_step, 1)
                dve.wait_ge(max_step, p * 6 + 5)
                dve.tensor_tensor(sm["smax"][:], sm["mx1"][:], sm["cq"][:, ds(p, 1)], ALU.add).then_inc(max_step, 1)
                dve.wait_ge(max_step, p * 6 + 6)
                if not (isinstance(p, int) and p == 0):
                    dve.wait_ge(exp_done, p * NCH)
                dve.tensor_tensor(sm["ebias"][:], sm["cq"][:, ds(p, 1)], sm["smax"][:], ALU.subtract
                                  ).then_inc(ebias_ok, 1)

            def denominators(p):
                dve.wait_ge(den_mm, p + 1)
                dve.tensor_copy(sm["den"][:], ps[:, TRB, 0:1]).then_inc(den_ok, 1)
                dve.wait_ge(den_ok, p * 2 + 1)
                dve.tensor_scalar(sm["den1"][:], sm["den"][:], EPS_DEN, None, ALU.add).then_inc(den_ok, 1)
                dve.wait_ge(den_ok, p * 2 + 2)
                dve.reciprocal(sm["rden"][:], sm["den1"][:]).then_inc(rden_ok, 1)

            def finish_pair(p):
                dve.wait_ge(part_mm, p + 1)
                dve.scalar_tensor_tensor(out=tmp[:], in0=bwe_b[:], scalar=sm["den"][:, 0:1], in1=ps[:, OUT, :],
                                         op0=ALU.mult, op1=ALU.add).then_inc(tmp_ok, 1)
                dve.wait_ge(rden_ok, p + 1)
                dve.wait_ge(tmp_ok, p + 1)
                dve.scalar_tensor_tensor(out=row(p), in0=tmp[:], scalar=sm["rden"][:, 0:1], in1=row(p),
                                         op0=ALU.mult, op1=ALU.add).then_inc(x2_ok, 1)
                dve.wait_ge(x2_ok, p + 1)
                dve.wait_ge(x_all_in, 16)
                dve.bn_stats(sm["st3"][:, ds(p * 6, 6)], row(p)).then_inc(st3_ok, 1)

            def low_norm_t(p):
                dve.wait_ge(n_hi, p + 1)
                dve.tensor_tensor(nt_lo[:], ps[:, TRA, :].rearrange("p (k n) -> p k n", k=KD),
                                  nt_hi[:].bitcast(F32), ALU.subtract).then_inc(n_lo, 1)

            def copy_qk(p):
                dve.wait_ge(qk_mm, p + 1)
                if not (isinstance(p, int) and p == 0):
                    dve.wait_ge(z_ok, p * 2)
                for b in range(BP):
                    dve.tensor_copy(q2[b * A:(b + 1) * A, :], ps[0:A, TRB, b * SQ:(b + 1) * SQ])
                    ins = dve.tensor_copy(k2[b * A:(b + 1) * A, :], ps[A:2 * A, TRB, b * SQ:(b + 1) * SQ])
                ins.then_inc(qk_ok, 1)

            def relu_half(p, h):
                dve.wait_ge(z_ok, p * 2 + h + 1)
                v = plane[:, h * 2048:(h + 1) * 2048]
                dve.tensor_scalar(v, v, 0.0, None, ALU.max).then_inc(relu_ok, 1)

            def copy_probs_t(p):
                for g in (0, 2):
                    lo, hi = GROUPS[g]
                    dve.wait_ge(probs_tr, p * 4 + g + 1)
                    dve.tensor_copy(probs_t[:, lo:hi, :],
                                    ps[:, TRA, 0:(hi - lo) * P].rearrange("p (k n) -> p k n", n=P)).then_inc(pt_dve, 1)

            def normalise(p):
                dve.wait_ge(exp_done, p * NCH + NCH)
                dve.reduce_sum(sm["ssum"][:], sm["sums"][:], AX.X).then_inc(rinv_step, 1)
                dve.wait_ge(rinv_step, p * 2 + 1)
                dve.reciprocal(sm["rinv"][:], sm["ssum"][:]).then_inc(rinv_step, 1)
                dve.wait_ge(rinv_step, p * 2 + 2)
                dve.wait_ge(pv_done, p * 4 + 4)
                dve.tensor_scalar(norm[:], ps[:, OUT, :], sm["rinv"][:, 0:1], None, ALU.mult).then_inc(attended_ok, 1)

            def low_o_t(p):
                dve.wait_ge(o_hi, p + 1)
                dve.tensor_tensor(nt_lo[:], ps[:, TRA, :].rearrange("p (k n) -> p k n", k=KD),
                                  nt_hi[:].bitcast(F32), ALU.subtract).then_inc(o_lo, 1)

            def pairwise_softmax(p):
                dve.wait_ge(s16_mm, p + 1)
                v = ps[:, TRB, :].rearrange("p (i j) -> p i j", j=SQ)
                dve.reduce_max(sm["mx16"][:], v, AX.X).then_inc(s16_max, 1)
                dve.wait_ge(s16_max, p + 1)
                dve.tensor_tensor(ex[:, :].rearrange("p (i j) -> p i j", j=SQ), v,
                                  sm["mx16"][:, :].unsqueeze(2).to_broadcast([P, 8, SQ]), ALU.subtract
                                  ).then_inc(s16_sub, 1)

            def parts_of_ex(p):
                dve.wait_ge(ex_hi_ok, p + 1)
                dve.scalar_tensor_tensor(out=ex_parts[:], in0=ex_hi[:].bitcast(F32), scalar=sm["minus_low"][:, 0:1],
                                         in1=ex[:], op0=ALU.mult, op1=ALU.add).then_inc(ex_parts_ok, 1)

            def add_x(p):
                dve.wait_ge(vproj, p + 1)
                dve.wait_ge(xb_ready, p + 1)
                dve.wait_ge(q_ready, p + 1)
                dve.tensor_tensor(row(p), ps[:, ACC, :], x_in[:], ALU.add).then_inc(x1_ok, 1)

            def stats2(p):
                wait_apart(dve, x1_ok, p + 1)
                dve.bn_stats(sm["st2"][:], row(p)).then_inc(ln2_stat, 1)
                wait_apart(dve, ln2_stat, p * 2 + 1)
                dve.bn_aggr(sm["mv2"][:], sm["st2"][:]).then_inc(ln2_stat, 1)

            def norm2(p):
                dve.wait_ge(ln2_sd, p + 1)
                dve.reciprocal(sm["rs2"][:], sm["sd2"][:]).then_inc(ln2_rs, 1)
                dve.wait_ge(ln2_rs, p + 1)
                dve.tensor_scalar(norm[:], row(p), sm["mv2"][:, 0:1], sm["rs2"][:, 0:1], ALU.subtract, ALU.mult
                                  ).then_inc(ln2_ok, 1)

            def gather_ex_t(p):
                dve.wait_ge(ex_tr, p + 1)
                for b in range(BP):
                    for par in range(2):
                        dst = ex_t[b * SQ:(b + 1) * SQ, b * SQ:(b + 1) * SQ].rearrange(
                            "p (g j m s) -> p g j m s", g=2, j=4, m=4)[:, :, :, :, par]
                        src = ps[par * SQ:(par + 1) * SQ, TRB, :].rearrange(
                            "p (m j r) -> p r j m", m=4, j=4)[:, b:b + 3:2, :, :]
                        ins = dve.tensor_copy(dst, src)
                ins.then_inc(ex_t_ok, 1)

            def products(p, lo, hi):
                for c in range(lo, hi):
                    dve.wait_ge(spread, p * NC8 + c + 1)
                    v = plane[:, c * 512:(c + 1) * 512]
                    dve.scalar_tensor_tensor(out=v, in0=v, scalar=-ROOT_EPS_RHO, in1=ps[:, c % 4, :],
                                             op0=ALU.add, op1=ALU.mult).then_inc(prod, 1)

            def sum_products(p, half):
                dve.wait_ge(prod, p * NC8 + (half + 1) * NC8 // 2)
                h = SQ // 2
                dve.reduce_sum(ew[:, half * h:(half + 1) * h],
                               plane[:, half * h * SQ:(half + 1) * h * SQ].rearrange("p (i j) -> p i j", j=SQ),
                               AX.X).then_inc(ew_red, 1)

            def place_sums(p):
                dve.wait_ge(ew_red, p * 2 + 2)
                for b in range(BP):
                    ins = dve.tensor_copy(ew_t[b * A:(b + 1) * A, b * SQ:(b + 1) * SQ], ew[b * A:(b + 1) * A, :])
                ins.then_inc(ew_ok, 1)

            def stats3(lo, hi):
                dve.wait_ge(st3_ok, hi)
                for t in range(lo, hi):
                    dve.bn_aggr(sm["mv3"][:, 2 * t:2 * t + 2], sm["st3"][:, 6 * t:6 * t + 6]).then_inc(ln3_stat, 1)

            def inverse3(lo, hi):
                part = 1 if lo == 0 else 2
                dve.wait_ge(ln3_sd, part)
                dve.reciprocal(sm["rs3"][:, lo:hi], sm["sd3"][:, lo:hi]).then_inc(ln3_rs, 1)
                dve.wait_ge(ln3_rs, part)

            def apply3(t):
                if t == 0:
                    dve.wait_ge(probs_tr, NP * 4)
                if t >= 2:
                    dve.wait_ge(x3_tr, t - 1)
                dve.tensor_scalar(n3[t % 2][:], rows3[:, t, :], sm["mv3"][:, 2 * t:2 * t + 1], sm["rs3"][:, t:t + 1],
                                  ALU.subtract, ALU.mult).then_inc(ln3_ok, 1)

            def low_x3(t):
                dve.wait_ge(x3_hi_ok, t + 1)
                dve.tensor_tensor(x3_part(x3_lo, t), x3_bank(t), x3_part(x3_hi, t).bitcast(F32), ALU.subtract
                                  ).then_inc(x3_lo_ok, 1)

            def gated(s):
                for n in range(2):
                    dve.wait_ge(silu_ok, s * 2 + n + 1)
                    if not (isinstance(s, int) and s == 0):
                        dve.wait_ge(h_lo_ok, s * 2 - 1 + n)
                    dve.tensor_tensor(h_sb[:, n, :], silu_sb[:, n, :], ps[:, 2 * n + 1, :], ALU.mult).then_inc(h_ok, 1)

            def low_h(s, u):
                for n in range(2):
                    dve.wait_ge(h_hi_ok, s * 2 + n + 1)
                    dve.tensor_tensor(h_lo[u][:, n, :], h_sb[:, n, :], h_hi[u][:, n, :].bitcast(F32), ALU.subtract
                                      ).then_inc(h_lo_ok, 1)

            def both(t, pairwise, ending):
                chunk_max(t, 0)
                chunk_max(t, 1)
                chunk_max(t, 2)
                if ending:
                    denominators(t - 2)
                    finish_pair(t - 2)
                if last_pair(t):
                    stats3(0, EARLY3)
                if pairwise:
                    low_norm_t(t - 1)
                chunk_max(t, 3)
                row_max(t)
                if pairwise:
                    copy_qk(t - 1)
                copy_probs_t(t)
                if pairwise:
                    relu_half(t - 1, 0)
                    relu_half(t - 1, 1)
                if last_pair(t):
                    inverse3(0, EARLY3)
                    apply3(0)
                    apply3(1)
                    low_x3(0)
                    apply3(2)
                if pairwise:
                    pairwise_softmax(t - 1)
                    parts_of_ex(t - 1)
                    gather_ex_t(t - 1)
                if last_pair(t):
                    low_x3(1)
                    apply3(3)
                if pairwise:
                    products(t - 1, 0, 4)
                if last_pair(t):
                    low_x3(2)
                normalise(t)
                if pairwise:
                    products(t - 1, 4, 6)
                low_o_t(t)
                if pairwise:
                    products(t - 1, 6, NC8)
                    sum_products(t - 1, 0)
                add_x(t)
                if last_pair(t):
                    low_x3(3)
                stats2(t)
                if last_pair(t):
                    apply3(4)
                norm2(t)
                if pairwise:
                    sum_products(t - 1, 1)
                    place_sums(t - 1)

            both(0, False, False)
            both(1, True, False)
            with dve.Fori(LOOP, NP - 1) as t:
                both(t, True, True)
            both(NP - 1, True, True)

            denominators(NP - 2)
            low_norm_t(NP - 1)
            copy_qk(NP - 1)
            relu_half(NP - 1, 0)
            relu_half(NP - 1, 1)
            apply3(5)
            finish_pair(NP - 2)
            low_x3(4)
            dve.wait_ge(gate_split_hi, 1)
            dve.tensor_tensor(gate_lo[:], gate_sb[:], gate_hi[:].bitcast(F32), ALU.subtract).then_inc(gate_split_lo, 1)
            gated(0)
            pairwise_softmax(NP - 1)
            low_h(0, 0)
            parts_of_ex(NP - 1)
            gather_ex_t(NP - 1)
            products(NP - 1, 0, 4)
            low_x3(5)
            products(NP - 1, 4, NC8)
            sum_products(NP - 1, 0)
            sum_products(NP - 1, 1)
            place_sums(NP - 1)
            denominators(NP - 1)
            finish_pair(NP - 1)
            stats3(EARLY3, NP)
            inverse3(EARLY3, NP)
            apply3(6)
            apply3(7)
            gated(1)
            low_x3(6)
            low_x3(7)
            low_h(1, 1)

            dve.wait_ge(logit_tr, 1)
            dve.tensor_copy(sm["logits"][:], ps[:, TRA, 0:NP * E]).then_inc(logits_ok, 1)
            dve.wait_ge(score_ok, 1)
            steps = [0]

            def link(ins):
                ins.then_inc(gate_step, 1)
                steps[0] += 1
                dve.wait_ge(gate_step, steps[0])

            G = E // 2

            def v3(name, n):
                return sm[name][:, :].rearrange("p (t e) -> p t e", e=n)

            def beaten(out_name, in_name, n):
                mine = v3(in_name, n).unsqueeze(3).to_broadcast([P, NP, n, n])
                other = v3(in_name, n).unsqueeze(2).to_broadcast([P, NP, n, n])
                first = sm["before"][:, :].rearrange("p (e f) -> p e f", e=E)[:, 0:n, 0:n].unsqueeze(1).to_broadcast(
                    [P, NP, n, n])
                link(dve.tensor_tensor(tie[:, :, 0:n, 0:n], mine, other, ALU.is_equal))
                for q in range(NP):
                    ins = dve.tensor_tensor(tie[:, q, 0:n, 0:n], tie[:, q, 0:n, 0:n], first[:, q], ALU.mult)
                link(ins)
                link(dve.tensor_tensor(beat[:, :, 0:n, 0:n], other, mine, ALU.is_gt))
                link(dve.tensor_tensor(beat[:, :, 0:n, 0:n], beat[:, :, 0:n, 0:n], tie[:, :, 0:n, 0:n], ALU.add))
                link(dve.reduce_sum(v3(out_name, n), beat[:, :, 0:n, 0:n], AX.X))

            link(dve.tensor_tensor(v3("choice", E), v3("score", E),
                                   sm["gbias"][:, :].unsqueeze(1).to_broadcast([P, NP, E]), ALU.add))
            pairs_of = sm["choice"][:, :].rearrange("p (t g e) -> p t g e", g=G, e=2)
            link(dve.tensor_tensor(v3("grp", G), pairs_of[:, :, :, 0], pairs_of[:, :, :, 1], ALU.add))
            beaten("grank", "grp", G)
            link(dve.tensor_scalar(sm["gmask"][:], sm["grank"][:], 2.0, None, ALU.is_lt))
            link(dve.tensor_tensor(sm["kept"][:, :].rearrange("p (t g e) -> p (t g) e", g=G, e=2),
                                   sm["choice"][:, :].rearrange("p (t g e) -> p (t g) e", g=G, e=2),
                                   sm["gmask"][:, :].unsqueeze(2).to_broadcast([P, NP * G, 2]), ALU.mult))
            link(dve.tensor_scalar(sm["kept"][:], sm["kept"][:], 0.0, None, ALU.add))
            beaten("rank", "kept", E)
            link(dve.tensor_scalar(sm["rank"][:], sm["rank"][:], 2.0, None, ALU.is_lt))
            link(dve.tensor_tensor(sm["wsel"][:], sm["score"][:], sm["rank"][:], ALU.mult))
            link(dve.reduce_sum(sm["wsum"][:], v3("wsel", E), AX.X))
            link(dve.tensor_scalar(sm["wsum"][:], sm["wsum"][:], EPS_TOPK, None, ALU.add))
            link(dve.reciprocal(sm["winv"][:], sm["wsum"][:]))
            link(dve.tensor_tensor(sm["comb"][:, :].rearrange("p (e t) -> p t e", e=E), v3("wsel", E),
                                   sm["winv"][:, :].unsqueeze(2).to_broadcast([P, NP, E]), ALU.mult))

            comb_e = [sm["comb_e0"], sm["comb_e1"]]

            def add_step(s, h, slot):
                for j in range(4):
                    r = rows3[:, h * 4 + j, :]
                    dve.wait_ge(down_mm, s * 4 + j + 1)
                    share = comb_e[slot][:, h * 4 + j:h * 4 + j + 1]
                    dve.scalar_tensor_tensor(out=r, in0=ps[:, 4 + j, :], scalar=share, in1=r, op0=ALU.mult, op1=ALU.add).then_inc(y_ok, 1)

            def four(e2, first, last):
                if not first:
                    dve.wait_ge(y_ok, e2 * 16)
                for s in range(2):
                    dve.tensor_copy(comb_e[s][:], sm["comb"][:, ds(e2 * (2 * NP) + s * NP, NP)]).then_inc(comb_ok, 1)
                dve.wait_ge(comb_ok, e2 * 2 + 2)
                for u in range(4):
                    if not (first and u == 0 or last and u == 3):
                        gated(e2 * 4 + u + 1)
                        low_h(e2 * 4 + u + 1, (u + 1) % 2)
                    add_step(e2 * 4 + u, u // 2, u % 2)

            four(0, True, False)
            with dve.Fori(1, E // 2 - 1) as e2:
                four(e2, False, False)
            four(E // 2 - 1, False, True)

        @block.tensor
        def _(pe):
            for k in range(KD):
                pe.wait_ge(wqk_in[k], 32)
                for m in range(KD):
                    ins = pe.matmul(ps[:, m, :], wq_sb[:, k, m * P:(m + 1) * P], wk_sb[:, k, :], start=(k == 0),
                                    stop=(k == KD - 1))
                    if k == KD - 1:
                        ins.then_inc(m_mm, 1)

            def turn_rows(t):
                pe.wait_ge(ln1_ok, t + 1)
                if t >= 2:
                    pe.wait_ge(ln1_lo, t - 1)
                for k in range(KD):
                    ins = pe.transpose(ps[:, OUT + t % 2, k * P:(k + 1) * P], rows3[:, t, k * P:(k + 1) * P], ident[:])
                ins.then_inc(ln1_tr, 1)

            def wk_bias(m):
                for k in range(KD):
                    ins = pe.matmul(ps[:, TRB, m * P:(m + 1) * P], wk_sb[:, k, m * P:(m + 1) * P], bq_rep[:, k, :],
                                    start=(k == 0), stop=(k == KD - 1))
                if m == KD - 1:
                    ins.then_inc(bias_mm, 1)

            pe.wait_ge(bk_rep_ok, 1)
            pe.wait_ge(pool_const, POOL_CONSTS)
            for k in range(KD):
                ins = pe.matmul(ps[:, TRA, :], bk_rep[:, k, :], wq_sb[:, k, :], start=(k == 0), stop=(k == KD - 1))
            ins.then_inc(vrep_mm, 1)
            turn_rows(0)
            turn_rows(1)
            wk_bias(0)
            turn_rows(2)
            wk_bias(1)
            turn_rows(3)
            wk_bias(2)
            turn_rows(4)
            wk_bias(3)
            turn_rows(5)
            pe.wait_ge(bias_ok, 1)
            for k in range(KD):
                ins = pe.matmul(ps[:, TRA, 0:P], bk_rep[:, k, :], bq_rep[:, k, :], start=(k == 0), stop=(k == KD - 1))
            ins.then_inc(bias_mm, 1)
            turn_rows(6)
            turn_rows(7)
            pe.wait_ge(m_lo_ok, KD)
            for h, (hi, lo) in enumerate(((x1t_hi, x1t_lo), (x1t_hi2, x1t_lo2))):
                pe.wait_ge(ln1_lo, 4 * h + 4)
                if h:
                    pe.wait_ge(bias_ok, 3)
                for m in range(KD):
                    for k in range(KD):
                        ins = split3(pe, ps[:, 4 * h + m, :], m_hi[:, k, m * P:(m + 1) * P],
                                     m_lo[:, k, m * P:(m + 1) * P], hi[:, k, :], lo[:, k, :], k == 0, k == KD - 1)
                    ins.then_inc(q_mm, 1)

            def scores(p, chunks):
                if 0 in chunks:
                    pe.wait_ge(q_ready, p + 1)
                for c in chunks:
                    pe.wait_ge(keys_in[c], p * 16 + 16)
                    if isinstance(p, int) and p == 0:
                        pe.wait_ge(q_ok, c + 1)
                    elif isinstance(p, int) and p == 1:
                        pe.wait_ge(exp_done, c + 1)
                    else:
                        pe.wait_ge(prod, p * NC8 - 2 * NC8 + c + 5)
                    for k in range(KD):
                        for b in range(BP):
                            ins = pe.matmul(ps[b * SQ:(b + 1) * SQ, c, 0:width(c)],
                                            q_cur[:, k, b * SQ:(b + 1) * SQ], keys[:, c, b * KD + k, 0:width(c)],
                                            start=(k == 0), stop=(k == KD - 1))
                    ins.then_inc(scored, 1)

            def first_part(p):
                pe.wait_ge(ex_t_ok, p + 1)
                pe.matmul(ps[:, TRB, 0:2], ex_t[:], small["ones"][:], start=True, stop=True).then_inc(den_mm, 1)
                if not (isinstance(p, int) and p == NP - 1):
                    pe.wait_ge(attended_ok, p + 2)
                pe.wait_ge(vy_ok, p + 1)
                pe.matmul(ps[:, OUT, :], ex_t[:], vy[:], start=True, stop=False)

            def second_part(p):
                pe.wait_ge(ew_ok, p + 1)
                pe.matmul(ps[:, OUT, :], ew_t[:], we2[:], start=False, stop=True).then_inc(part_mm, 1)

            def norm_t(p):
                pe.wait_ge(ln2_ok, p + 1)
                pe.wait_ge(o_lo, p + 1)
                for k in range(KD):
                    ins = pe.transpose(ps[:, TRA, k * P:(k + 1) * P], norm[:, k * P:(k + 1) * P], ident[:])
                ins.then_inc(n_tr, 1)

            def pairwise_qk(p):
                pe.wait_ge(n_f, p + 1)
                if not (isinstance(p, int) and p == 0):
                    pe.wait_ge(den_ok, p * 2)
                else:
                    pe.wait_ge(pt_act, 2)
                for k in range(KD):
                    ins = pe.matmul(ps[:, TRB, 0:P], wqk_sb[:, k, :], nt_f[:, k, :], start=(k == 0),
                                    stop=(k == KD - 1))
                ins.then_inc(qk_mm, 1)

            def values_y(p):
                pe.wait_ge(n_lo, p + 1)
                pe.wait_ge(x1_ok, p + 1)
                if isinstance(p, int) and p == 0:
                    pe.wait_ge(wsplit_lo, 2)
                for k in range(KD):
                    ins = split3(pe, ps[:, ACC, :], nt_hi[:, k, :], nt_lo[:, k, :], wy_hi[:, k, :], wy_lo[:, k, :],
                                 k == 0, k == KD - 1)
                ins.then_inc(vy_mm, 1)

            def turn_probs(p, pairwise):
                for g, (lo, hi) in enumerate(GROUPS):
                    if g < 3:
                        pe.wait_ge(exp_done, p * NCH + -(-hi * P // CW))
                    if g == 0 and not pairwise:
                        pe.wait_ge(q_ok, 2 * KD)
                    if g == 0 and pairwise:
                        pe.wait_ge(n_lo, p)
                    if g == 1 and pairwise:
                        pe.wait_ge(qk_ok, p)
                    if g == 2:
                        pe.wait_ge(pt_dve, p * 2 + 1)
                    if g == 3:
                        pe.wait_ge(pt_act, p * 2 + 1)
                    for n in range(lo, hi):
                        w = P if n < NT - 1 else TAIL
                        ins = pe.transpose(ps[0:w, TRA + g % 2, (n - lo) * P:(n - lo + 1) * P],
                                           probs[:, n * P:n * P + w], ident[:])
                    ins.then_inc(probs_tr, 1)

            def attend(p, g, tiles=None):
                lo, hi = GROUPS[g] if tiles is None else tiles
                if g % 2 == 0:
                    pe.wait_ge(pt_dve, p * 2 + g // 2 + 1)
                else:
                    pe.wait_ge(pt_act, p * 2 + g // 2 + 1)
                if g == 0 and not (isinstance(p, int) and p < 2):
                    pe.wait_ge(tmp_ok, p - 1)
                pe.wait_ge(vals_in[g], (p + 1) * (64 if GROUPS[g][1] == NT else 32))
                for n in range(lo, hi):
                    w = P if n < NT - 1 else TAIL
                    for b in range(BP):
                        ins = pe.matmul(ps[b * SQ:(b + 1) * SQ, OUT, :], probs_t[0:w, n, b * SQ:(b + 1) * SQ],
                                        vals[0:w, n % RING, b, :], start=(n == 0), stop=(n == NT - 1))
                if hi == GROUPS[g][1]:
                    ins.then_inc(pv_done, 1)

            def turn_attended(p):
                pe.wait_ge(attended_ok, p + 1)
                if last_pair(p):
                    pe.wait_ge(x3_lo_ok, 3)
                for k in range(KD):
                    ins = pe.transpose(ps[:, TRA, k * P:(k + 1) * P], norm[:, k * P:(k + 1) * P], ident[:])
                ins.then_inc(o_tr, 1)

            def pairwise_scores(p):
                if isinstance(p, int) and p == 0:
                    pe.wait_ge(phi_ok, 8)
                if not (isinstance(p, int) and p == NP - 1):
                    pe.wait_ge(pt_act, p * 2 + 4)
                for c in range(NC8):
                    if c % 4 == 0:
                        pe.wait_ge(root_ok, p * 2 + c // 4 + 1)
                    j = c % 4
                    ins = pe.matmul(ps[32 * j:32 * j + 32, TRB, :], phi_sel[:, c // 4, :],
                                    plane[:, c * 512:(c + 1) * 512], start=(c < 4), stop=(c >= 4))
                ins.then_inc(s16_mm, 1)

            def project(p):
                pe.wait_ge(o_hi, p + 1)
                if isinstance(p, int) and p == 0:
                    pe.wait_ge(wsplit_lo, 1)
                else:
                    pe.wait_ge(vy_ok, p)
                for k in range(KD):
                    pe.matmul(ps[:, ACC, :], nt_hi[:, k, :], wv_hi[:, k, :], start=(k == 0), stop=False)
                    pe.matmul(ps[:, ACC, :], nt_hi[:, k, :], wv_lo[:, k, :], start=False, stop=False)
                pe.wait_ge(o_lo, p + 1)
                for k in range(KD):
                    ins = pe.matmul(ps[:, ACC, :], nt_lo[:, k, :], wv_hi[:, k, :], start=False, stop=(k == KD - 1))
                ins.then_inc(vproj, 1)

            def turn_ex(p):
                pe.wait_ge(s16_exp, p + 1)
                for m in range(4):
                    ins = pe.transpose(ps[:, TRB, m * P:(m + 1) * P], ex[:, m * P:(m + 1) * P], ident[:])
                ins.then_inc(ex_tr, 1)

            def spread_ex(p, half):
                if half == 0:
                    pe.wait_ge(ex_parts_ok, p + 1)
                    if last_pair(p):
                        pe.wait_ge(h_ok, 2)
                    else:
                        pe.wait_ge(exp_done, p * NCH + 2 * NCH)
                if isinstance(p, int) and p == 0:
                    pe.wait_ge(sel_ok, 1)
                for c in range(4 * half, 4 * half + 4):
                    if c >= 4:
                        pe.wait_ge(prod, p * NC8 + c - 3)
                    pe.matmul(ps[:, c % 4, :], sel[:, c, :], ex_parts[:], start=True, stop=True).then_inc(spread, 1)

            def turn_x3(t):
                pe.wait_ge(ln3_ok, t + 1)
                free, count = {0: (pt_dve, 2 * NP), 1: (vy_ok, NP - 1), 2: (x3_lo_ok, 1), 3: (prod, (NP - 1) * NC8),
                               4: (n_lo, NP), 5: (x3_lo_ok, 5), 6: (x3_lo_ok, 6), 7: (den_ok, 2 * NP)}[t]
                pe.wait_ge(free, count)
                for k in range(KD):
                    ins = pe.transpose(ps[:, X3_BANK[t], k * P:(k + 1) * P], n3[t % 2][:, k * P:(k + 1) * P], ident[:])
                ins.then_inc(x3_tr, 1)

            def gate_up_block(n, which, h, slot):
                col = which * I + n * P
                for k in range(KD):
                    wc = k * I2 + col
                    ins = split3(pe, ps[:, 2 * n + which, :], w_hi[slot][:, wc:wc + P], w_lo[slot][:, wc:wc + P],
                                 x3_hi[h][:, k, :], x3_lo[h][:, k, :], k == 0, k == KD - 1)
                if which == 1:
                    ins.then_inc(gu_mm, 1)

            def both(t, pairwise, ending):
                scores(t, (0, 1, 2))
                if ending:
                    second_part(t - 2)
                if pairwise:
                    norm_t(t - 1)
                scores(t, (3,))
                if pairwise:
                    pairwise_qk(t - 1)
                    values_y(t - 1)
                turn_probs(t, pairwise)
                attend(t, 0)
                attend(t, 1)
                if last_pair(t):
                    turn_x3(0)
                if pairwise:
                    pairwise_scores(t - 1)
                attend(t, 2)
                if last_pair(t):
                    turn_x3(1)
                if pairwise:
                    turn_ex(t - 1)
                attend(t, 3, (GROUPS[3][0], GROUPS[3][0] + 1))
                if pairwise:
                    spread_ex(t - 1, 0)
                if last_pair(t):
                    turn_x3(2)
                attend(t, 3, (GROUPS[3][0] + 1, NT))
                if pairwise:
                    spread_ex(t - 1, 1)
                turn_attended(t)
                if pairwise:
                    first_part(t - 1)
                project(t)

            both(0, False, False)
            both(1, True, False)
            with pe.Fori(LOOP, NP - 1) as t:
                both(t, True, True)
            both(NP - 1, True, True)

            turn_x3(3)
            pe.wait_ge(w_lo_ok, 1)
            pe.wait_ge(x3_lo_ok, 4)
            gate_up_block(0, 0, 0, 0)
            norm_t(NP - 1)
            pairwise_qk(NP - 1)
            gate_up_block(0, 1, 0, 0)
            second_part(NP - 2)
            values_y(NP - 1)
            gate_up_block(1, 0, 0, 0)
            gate_up_block(1, 1, 0, 0)
            turn_x3(4)
            pairwise_scores(NP - 1)

            def logits(h):
                pe.wait_ge(x3_hi_ok, 4 * h + 4)
                if h == 0:
                    pe.wait_ge(gate_split_lo, 1)
                    pe.wait_ge(vy_ok, NP)
                else:
                    pe.wait_ge(tmp_ok, NP)
                for k in range(KD):
                    pe.matmul(ps[:, ACC - h, :], gate_hi[:, k, :], x3_hi[h][:, k, :], start=(k == 0), stop=False)
                    pe.matmul(ps[:, ACC - h, :], gate_lo[:, k, :], x3_hi[h][:, k, :], start=False, stop=False)
                pe.wait_ge(x3_lo_ok, 4 * h + 4)
                for k in range(KD):
                    ins = pe.matmul(ps[:, ACC - h, :], gate_hi[:, k, :], x3_lo[h][:, k, :], start=False,
                                    stop=(k == KD - 1))
                ins.then_inc(logit_mm, 1)

            logits(0)
            turn_x3(5)
            turn_ex(NP - 1)
            spread_ex(NP - 1, 0)
            spread_ex(NP - 1, 1)
            first_part(NP - 1)
            pe.wait_ge(w_lo_ok, 2)
            pe.wait_ge(prod, (NP - 1) * NC8 + 6)
            gate_up_block(0, 0, 0, 1)
            gate_up_block(0, 1, 0, 1)
            second_part(NP - 1)
            pe.wait_ge(prod, NP * NC8)
            gate_up_block(1, 0, 0, 1)
            gate_up_block(1, 1, 0, 1)
            turn_x3(6)
            turn_x3(7)
            logits(1)

            def turn_logits():
                pe.wait_ge(logit_ok, 2)
                for t in range(NP):
                    ins = pe.transpose(ps[:, TRA, t * E:(t + 1) * E], logit_t[:, t * P:(t + 1) * P], ident[0:E, 0:E])
                ins.then_inc(logit_tr, 1)

            turn_logits()

            def gate_up(s, u, split):
                if u < 2:
                    pe.wait_ge(w_lo_ok, split)
                for n in range(2):
                    pe.wait_ge(h_ok, s * 2 - 1 + n)
                    for which in range(2):
                        gate_up_block(n, which, u // 2, u % 2)

            def down(s, u, split, first):
                if u < 2:
                    pe.wait_ge(w_lo_ok, split)
                pe.wait_ge(h_lo_ok, s * 2 + 2)
                for j in range(4):
                    if not first:
                        pe.wait_ge(y_ok, s * 4 - 3 + j)
                    elif j == 0:
                        pe.wait_ge(logits_ok, 1)
                    for n in range(2):
                        wc = KD * I2 + n * D
                        ins = split3(pe, ps[:, 4 + j, :], h_hi[u % 2][:, n, j * P:(j + 1) * P],
                                     h_lo[u % 2][:, n, j * P:(j + 1) * P], w_hi[u % 2][:, wc:wc + D],
                                     w_lo[u % 2][:, wc:wc + D], n == 0, n == 1)
                    ins.then_inc(down_mm, 1)

            def four(e2, first, last):
                for u in range(4):
                    if not (first and u == 0 or last and u == 3):
                        v = (u + 1) % 4
                        gate_up(e2 * 4 + u + 1, v, e2 * 4 + (2 if v == 1 else 5))
                    down(e2 * 4 + u, u, e2 * 4 + 3 + u % 2, first and u == 0)

            four(0, True, False)
            with pe.Fori(1, E // 2 - 1) as e2:
                four(e2, False, False)
            four(E // 2 - 1, False, True)


def kernel(**inputs):
    import numpy as np
    import concourse.bacc as bacc
    from concourse.bass_utils import run_bass_kernel_spmd

    def laid(a):
        return np.ascontiguousarray(a)

    i = {k: np.asarray(v) for k, v in inputs.items()}
    arrays = {
        "x": laid(i["x"]),
        "ctx": laid(i["ctx_1024"]),
        "ctx_t": laid(i["ctx_1024"].transpose(0, 2, 1)),
        "wq": laid(i["L0_xattn_Wq"]),
        "bq": laid(i["L0_xattn_bq"].reshape(-1, P).T),
        "wk": laid(i["L0_xattn_Wk"]),
        "bk": laid(i["L0_xattn_bk"].reshape(-1, P).T),
        "wv_t": laid(i["L0_xattn_Wv"].T),
        "bv": laid(i["L0_xattn_bv"]),
        "wqk_t": laid(np.concatenate([i["L0_attn_Wq"], i["L0_attn_Wk"]], 0).T),
        "wphi": laid(i["L0_attn_Wphi"]),
        "wy_t": laid(i["L0_attn_Wy_w"].T),
        "wy_b": laid(i["L0_attn_Wy_b"]),
        "we_t": laid(i["L0_attn_We_w"].T),
        "we_b": laid(i["L0_attn_We_b"]),
        "gate_t": laid(i["L0_ffn_gate_weight"].T),
        "gate_bias": laid(i["L0_ffn_e_score_correction_bias"]),
        "gu_t": laid(np.concatenate([i["L0_ffn_gate_proj"], i["L0_ffn_up_proj"]], 1).transpose(0, 2, 1)),
        "down_t": laid(i["L0_ffn_down_proj"].transpose(0, 2, 1)),
    }
    nc = bacc.Bacc("TRN2", target_bir_lowering=False, num_devices=1)
    named = {f"in_{k}": v for k, v in arrays.items()}
    args = [nc.dram_tensor(k, v.shape, mybir.dt.from_np(v.dtype), kind="ExternalInput").ap() for k, v in named.items()]
    out = nc.dram_tensor("out_0", i["x"].shape, mybir.dt.float32, kind="ExternalOutput").ap()
    perceiver_kernel(nc, *args, out)
    r = run_bass_kernel_spmd(nc, [named], core_ids=[0])
    return r.results[0]["out_0"]
```
